# Optimizing a Trainium2 kernel written in Bass

```python
import numpy as np
import jax
import jax.numpy as jnp

def _softmax(x, axis=-1):
    return jax.nn.softmax(x, axis=axis)

def _gelu(x):
    return jax.nn.gelu(x, approximate=True)

def _silu(x):
    return jax.nn.silu(x)

def _sigmoid(x):
    return jax.nn.sigmoid(x)

def _layernorm(x, axis=-1, eps=1e-05):
    m = jnp.mean(x, axis=axis, keepdims=True)
    v = jnp.var(x, axis=axis, keepdims=True)
    return (x - m) / jnp.sqrt(v + eps)

def _scatter_add(tgt, idx, src, axis=0):
    return tgt.at[idx].add(src)

def _segment_sum(src, seg, n):
    return jax.ops.segment_sum(src, seg, n)
kernel_name = 'mk_dlrm_tower_d1_rec_r8_89283b'

def setup_inputs(seed: int=0):
    np.random.seed(seed)
    _w = jnp.asarray

    def _rec_inputs():
        import jax
        import jax.numpy as jnp
        _tk = jax.random.key(seed)
        ids = jnp.stack([jax.random.randint(jax.random.fold_in(_tk, 200 + f), (2048,), 0, v, jnp.int32) for f, v in enumerate([12500, 12500, 1000, 1250, 12500, 125000, 1000, 1250, 12500, 1000, 12500, 12500, 1250, 125000, 125000, 12500, 12500, 1000, 1000, 1000, 1250, 1000, 1250, 1250, 1000, 1000])], axis=1)
        tbl_0 = 0.05 * jax.random.normal(jax.random.fold_in(_tk, 500 + 0), (12500, 64), jnp.float32)
        tbl_1 = 0.05 * jax.random.normal(jax.random.fold_in(_tk, 500 + 1), (12500, 64), jnp.float32)
        tbl_2 = 0.05 * jax.random.normal(jax.random.fold_in(_tk, 500 + 2), (1000, 64), jnp.float32)
        tbl_3 = 0.05 * jax.random.normal(jax.random.fold_in(_tk, 500 + 3), (1250, 64), jnp.float32)
        tbl_4 = 0.05 * jax.random.normal(jax.random.fold_in(_tk, 500 + 4), (12500, 64), jnp.float32)
        tbl_5 = 0.05 * jax.random.normal(jax.random.fold_in(_tk, 500 + 5), (125000, 64), jnp.float32)
        tbl_6 = 0.05 * jax.random.normal(jax.random.fold_in(_tk, 500 + 6), (1000, 64), jnp.float32)
        tbl_7 = 0.05 * jax.random.normal(jax.random.fold_in(_tk, 500 + 7), (1250, 64), jnp.float32)
        tbl_8 = 0.05 * jax.random.normal(jax.random.fold_in(_tk, 500 + 8), (12500, 64), jnp.float32)
        tbl_9 = 0.05 * jax.random.normal(jax.random.fold_in(_tk, 500 + 9), (1000, 64), jnp.float32)
        tbl_10 = 0.05 * jax.random.normal(jax.random.fold_in(_tk, 500 + 10), (12500, 64), jnp.float32)
        tbl_11 = 0.05 * jax.random.normal(jax.random.fold_in(_tk, 500 + 11), (12500, 64), jnp.float32)
        tbl_12 = 0.05 * jax.random.normal(jax.random.fold_in(_tk, 500 + 12), (1250, 64), jnp.float32)
        tbl_13 = 0.05 * jax.random.normal(jax.random.fold_in(_tk, 500 + 13), (125000, 64), jnp.float32)
        tbl_14 = 0.05 * jax.random.normal(jax.random.fold_in(_tk, 500 + 14), (125000, 64), jnp.float32)
        tbl_15 = 0.05 * jax.random.normal(jax.random.fold_in(_tk, 500 + 15), (12500, 64), jnp.float32)
        tbl_16 = 0.05 * jax.random.normal(jax.random.fold_in(_tk, 500 + 16), (12500, 64), jnp.float32)
        tbl_17 = 0.05 * jax.random.normal(jax.random.fold_in(_tk, 500 + 17), (1000, 64), jnp.float32)
        tbl_18 = 0.05 * jax.random.normal(jax.random.fold_in(_tk, 500 + 18), (1000, 64), jnp.float32)
        tbl_19 = 0.05 * jax.random.normal(jax.random.fold_in(_tk, 500 + 19), (1000, 64), jnp.float32)
        tbl_20 = 0.05 * jax.random.normal(jax.random.fold_in(_tk, 500 + 20), (1250, 64), jnp.float32)
        tbl_21 = 0.05 * jax.random.normal(jax.random.fold_in(_tk, 500 + 21), (1000, 64), jnp.float32)
        tbl_22 = 0.05 * jax.random.normal(jax.random.fold_in(_tk, 500 + 22), (1250, 64), jnp.float32)
        tbl_23 = 0.05 * jax.random.normal(jax.random.fold_in(_tk, 500 + 23), (1250, 64), jnp.float32)
        tbl_24 = 0.05 * jax.random.normal(jax.random.fold_in(_tk, 500 + 24), (1000, 64), jnp.float32)
        tbl_25 = 0.05 * jax.random.normal(jax.random.fold_in(_tk, 500 + 25), (1000, 64), jnp.float32)
        _rk = jax.random.fold_in(_tk, 7)
        r_dense_t = 7.22013e-05 + 1.00017 * jax.random.normal(jax.random.fold_in(_rk, 101), (2048, 256), jnp.float32)
        W_top1 = 0.0360844 * jax.random.normal(jax.random.fold_in(_tk, 801), (768, 512), jnp.float32)
        W_top2 = 0.0441942 * jax.random.normal(jax.random.fold_in(_tk, 802), (512, 256), jnp.float32)
        W_top3 = 0.0625 * jax.random.normal(jax.random.fold_in(_tk, 803), (256, 1), jnp.float32)
        b_top1 = jnp.zeros((512,), jnp.float32)
        b_top2 = jnp.zeros((256,), jnp.float32)
        return (r_dense_t, ids, tbl_0, tbl_1, tbl_2, tbl_3, tbl_4, tbl_5, tbl_6, tbl_7, tbl_8, tbl_9, tbl_10, tbl_11, tbl_12, tbl_13, tbl_14, tbl_15, tbl_16, tbl_17, tbl_18, tbl_19, tbl_20, tbl_21, tbl_22, tbl_23, tbl_24, tbl_25, W_top1, b_top1, W_top2, b_top2, W_top3)
    r_dense_t, ids, tbl_0, tbl_1, tbl_2, tbl_3, tbl_4, tbl_5, tbl_6, tbl_7, tbl_8, tbl_9, tbl_10, tbl_11, tbl_12, tbl_13, tbl_14, tbl_15, tbl_16, tbl_17, tbl_18, tbl_19, tbl_20, tbl_21, tbl_22, tbl_23, tbl_24, tbl_25, W_top1, b_top1, W_top2, b_top2, W_top3 = _rec_inputs()

    def _L0_rec_setup():
        import jax, jax.numpy as jnp
        import numpy as np
        EPS = 1e-05
        NI = 33
        TRIL_I, TRIL_J = np.tril_indices(NI, k=-1)

        def layer_norm(x, g, b):
            m = jnp.mean(x, axis=-1, keepdims=True)
            v = jnp.mean(jnp.square(x - m), axis=-1, keepdims=True)
            return (x - m) * jax.lax.rsqrt(v + EPS) * g + b
        key = jax.random.key(seed)
        ks = jax.random.split(key, 8)
        B, D_DENSE, N_SP, D_SP = (4096, 256, 26, 64)
        E, PROJ, MAXD, NFLAT = (128, 32, 512, 528)
        dense_t = jax.random.normal(ks[0], (B, D_DENSE), dtype=jnp.float32)
        sparse_t = jax.random.normal(ks[1], (B, N_SP, D_SP), dtype=jnp.float32)
        Wd = jax.random.normal(ks[2], (E, D_DENSE), dtype=jnp.float32) / np.sqrt(D_DENSE)
        Ws = jax.random.normal(ks[3], (E, D_SP), dtype=jnp.float32) / np.sqrt(D_SP)
        Wsi = jax.random.normal(ks[4], (PROJ, N_SP), dtype=jnp.float32) / np.sqrt(N_SP)
        Wl = jax.random.normal(ks[5], (MAXD, NFLAT), dtype=jnp.float32) / np.sqrt(NFLAT)
        gd = jnp.ones((E,), jnp.float32)
        bd = jnp.zeros((E,), jnp.float32)
        gs = jnp.ones((E,), jnp.float32)
        bs = jnp.zeros((E,), jnp.float32)
        gsi = jnp.ones((PROJ,), jnp.float32)
        bsi = jnp.zeros((PROJ,), jnp.float32)
        gl = jnp.ones((MAXD,), jnp.float32)
        bl = jnp.zeros((MAXD,), jnp.float32)
        return {'dense_t': dense_t, 'sparse_t': sparse_t, 'Wd': Wd, 'gd': gd, 'bd': bd, 'Ws': Ws, 'gs': gs, 'bs': bs, 'Wsi': Wsi, 'gsi': gsi, 'bsi': bsi, 'Wl': Wl, 'gl': gl, 'bl': bl, 'dims_in_use': 384}
    _L0_rec_all = _L0_rec_setup()
    _L0_rec_in = {k: v for k, v in _L0_rec_all.items() if k in ('Wd', 'gd', 'bd', 'Ws', 'gs', 'bs', 'Wsi', 'gsi', 'bsi', 'Wl', 'gl', 'bl')}
    del _L0_rec_all
    return {'r_dense_t': r_dense_t, 'ids': ids, 'tbl_0': tbl_0, 'tbl_1': tbl_1, 'tbl_2': tbl_2, 'tbl_3': tbl_3, 'tbl_4': tbl_4, 'tbl_5': tbl_5, 'tbl_6': tbl_6, 'tbl_7': tbl_7, 'tbl_8': tbl_8, 'tbl_9': tbl_9, 'tbl_10': tbl_10, 'tbl_11': tbl_11, 'tbl_12': tbl_12, 'tbl_13': tbl_13, 'tbl_14': tbl_14, 'tbl_15': tbl_15, 'tbl_16': tbl_16, 'tbl_17': tbl_17, 'tbl_18': tbl_18, 'tbl_19': tbl_19, 'tbl_20': tbl_20, 'tbl_21': tbl_21, 'tbl_22': tbl_22, 'tbl_23': tbl_23, 'tbl_24': tbl_24, 'tbl_25': tbl_25, 'W_top1': W_top1, 'b_top1': b_top1, 'W_top2': W_top2, 'b_top2': b_top2, 'W_top3': W_top3, 'L0_rec_Wd': _L0_rec_in['Wd'], 'L0_rec_gd': _L0_rec_in['gd'], 'L0_rec_bd': _L0_rec_in['bd'], 'L0_rec_Ws': _L0_rec_in['Ws'], 'L0_rec_gs': _L0_rec_in['gs'], 'L0_rec_bs': _L0_rec_in['bs'], 'L0_rec_Wsi': _L0_rec_in['Wsi'], 'L0_rec_gsi': _L0_rec_in['gsi'], 'L0_rec_bsi': _L0_rec_in['bsi'], 'L0_rec_Wl': _L0_rec_in['Wl'], 'L0_rec_gl': _L0_rec_in['gl'], 'L0_rec_bl': _L0_rec_in['bl']}

def reference(r_dense_t, ids, tbl_0, tbl_1, tbl_2, tbl_3, tbl_4, tbl_5, tbl_6, tbl_7, tbl_8, tbl_9, tbl_10, tbl_11, tbl_12, tbl_13, tbl_14, tbl_15, tbl_16, tbl_17, tbl_18, tbl_19, tbl_20, tbl_21, tbl_22, tbl_23, tbl_24, tbl_25, W_top1, b_top1, W_top2, b_top2, W_top3, L0_rec_Wd, L0_rec_gd, L0_rec_bd, L0_rec_Ws, L0_rec_gs, L0_rec_bs, L0_rec_Wsi, L0_rec_gsi, L0_rec_bsi, L0_rec_Wl, L0_rec_gl, L0_rec_bl):
    import jax
    import jax.numpy as jnp

    def _L0_rec_ref(dense_t, sparse_t, Wd, gd, bd, Ws, gs, bs, Wsi, gsi, bsi, Wl, gl, bl, dims_in_use):
        import jax, jax.numpy as jnp
        import numpy as np
        EPS = 1e-05
        NI = 33
        TRIL_I, TRIL_J = np.tril_indices(NI, k=-1)

        def layer_norm(x, g, b):
            m = jnp.mean(x, axis=-1, keepdims=True)
            v = jnp.mean(jnp.square(x - m), axis=-1, keepdims=True)
            return (x - m) * jax.lax.rsqrt(v + EPS) * g + b
        x = layer_norm(dense_t @ Wd.T, gd, bd)
        y = layer_norm(jnp.einsum('bnd,ed->bne', sparse_t, Ws), gs, bs)
        y = jnp.einsum('bne,pn->bep', y, Wsi)
        y = layer_norm(y, gsi, bsi)
        y = jnp.swapaxes(y, 1, 2)
        T = jnp.concatenate([x[:, None, :], y], axis=1)
        Z = jnp.einsum('bnd,bmd->bnm', T, T)
        Zflat = Z[:, TRIL_I, TRIL_J]
        out = layer_norm(Zflat @ Wl.T, gl, bl)
        maxd = out.shape[-1]
        mask = (jnp.arange(maxd) < dims_in_use).astype(out.dtype)
        return out * mask
    e = jnp.stack([tbl_0[ids[:, 0]], tbl_1[ids[:, 1]], tbl_2[ids[:, 2]], tbl_3[ids[:, 3]], tbl_4[ids[:, 4]], tbl_5[ids[:, 5]], tbl_6[ids[:, 6]], tbl_7[ids[:, 7]], tbl_8[ids[:, 8]], tbl_9[ids[:, 9]], tbl_10[ids[:, 10]], tbl_11[ids[:, 11]], tbl_12[ids[:, 12]], tbl_13[ids[:, 13]], tbl_14[ids[:, 14]], tbl_15[ids[:, 15]], tbl_16[ids[:, 16]], tbl_17[ids[:, 17]], tbl_18[ids[:, 18]], tbl_19[ids[:, 19]], tbl_20[ids[:, 20]], tbl_21[ids[:, 21]], tbl_22[ids[:, 22]], tbl_23[ids[:, 23]], tbl_24[ids[:, 24]], tbl_25[ids[:, 25]]], axis=1)
    z = _L0_rec_ref(r_dense_t, e, L0_rec_Wd, L0_rec_gd, L0_rec_bd, L0_rec_Ws, L0_rec_gs, L0_rec_bs, L0_rec_Wsi, L0_rec_gsi, L0_rec_bsi, L0_rec_Wl, L0_rec_gl, L0_rec_bl, 384)
    z = z.reshape(z.shape[0], -1)
    h = jnp.concatenate([z, r_dense_t], axis=1)
    h = jnp.maximum(h @ W_top1 + b_top1, 0.0)
    h = jnp.maximum(h @ W_top2 + b_top2, 0.0)
    y = h @ W_top3
    return y

_drawn_inputs = setup_inputs


def setup_inputs(seed=0):
    import zlib

    import numpy as np

    out = dict(_drawn_inputs(seed))
    spreads = {'b_top1': (0.0, 0.1),
     'b_top2': (0.0, 0.1),
     'L0_rec_gd': (1.0, 0.6),
     'L0_rec_bd': (0.0, 0.8),
     'L0_rec_gs': (1.0, 0.6),
     'L0_rec_bs': (0.0, 0.1),
     'L0_rec_gsi': (1.0, 0.2),
     'L0_rec_bsi': (0.0, 0.1),
     'L0_rec_gl': (1.0, 0.2),
     'L0_rec_bl': (0.0, 0.1)}
    factors = {}
    for name, (base, spread) in spreads.items():
        noise = np.random.default_rng([zlib.crc32(name.encode()), seed]).standard_normal(out[name].shape)
        drawn = base * np.exp(spread * noise) if base else spread * noise
        out[name] = jnp.asarray(drawn.astype(out[name].dtype))
    for name, factor in factors.items():
        out[name] = (out[name] * factor).astype(out[name].dtype)
    return out
```

```python
from contextlib import ExitStack

import concourse.bass as bass
from concourse import mybir

BATCH = 2048
N_SPARSE = 26
D_SPARSE = 64
D_DENSE = 256
E_DIM = 128
PROJ = 32
N_FLAT = 528
MAXD = 512
DIMS_IN_USE = 384
H1, H2 = 512, 256
EPS = 1e-05

P = 128
BLK = 128
BLOCKS = BATCH // BLK
TILES = BLK * N_SPARSE // P
CHUNK = 64
CHUNK_TILES = CHUNK * N_SPARSE // P
UNIT = 32
UNITS = BLK // UNIT
BANK_B = 512 // PROJ
SPAN = -(-(P + N_SPARSE - 1) // N_SPARSE)
GROUPS = [(0, 8), (8, 14), (14, 20), (20, 26)]
ITEMS = PROJ + 2
GSLOTS = UNIT // 4
STEPS = 9
BODY = 2 * BLK
PASSES = BATCH // BODY
SLOTS = BODY // UNIT
O_CH = MAXD // P
Z_CH = DIMS_IN_USE // P
D_CH = D_DENSE // P
H2_CH = H2 // P
PACK_DMAS = 4 * 6


def tile_first(t):
    return t * P // N_SPARSE


def tile_last(t):
    return (t * P + P - 1) // N_SPARSE


def build_program(nc, table, ids, dense, size_c, base_c, eye, mask13, sel_row, sel_col,
                  wst2, gs_b, bs_row, wdt, gd_c, bd_c, wsi13, w9, ga, gb, bsi_cols, bsi_bq,
                  gl_c, bl_c, w1, b1_c, w2, b2_c, w3, out):
    fp32 = mybir.dt.float32
    i32 = mybir.dt.int32
    ALU = mybir.AluOpType
    ACT = mybir.ActivationFunctionType
    AX = mybir.AxisListType.X

    with ExitStack() as ctx:
        def sb(name, shape, dt=fp32):
            return ctx.enter_context(nc.sbuf_tensor(name, shape, dt))

        def ps(name, shape):
            return ctx.enter_context(nc.psum_tensor(name, shape, fp32))

        def sem(name):
            return ctx.enter_context(nc.semaphore(name))

        ids_raw = sb("ids_raw", [P, BLOCKS * TILES], i32)
        ids_f = sb("ids_f", [P, BLOCKS * TILES])
        ids_g = sb("ids_g", [P, BLOCKS * TILES])
        idx_all = sb("idx_all", [P, BLOCKS * TILES], i32)
        size_sb = sb("size_sb", [P, CHUNK_TILES])
        last_sb = sb("last_sb", [P, CHUNK_TILES])
        base_sb = sb("base_sb", [P, CHUNK_TILES])
        idx = [sb(f"idx{h}", [P, TILES], i32) for h in range(2)]
        rows = [sb(f"rows{h}", [P, TILES, D_SPARSE]) for h in range(2)]
        rows_n = [sb(f"rows_n{h}", [P, TILES, D_SPARSE]) for h in range(2)]
        rows_t = sb("rows_t", [P, 4 * P])
        prod = sb("prod", [P, 8 * D_SPARSE])
        row_var = sb("row_var", [P, 8])
        row_std = sb("row_std", [P, 8])
        row_inv = sb("row_inv", [P, 8])
        eye_sb = sb("eye_sb", [P, P])
        ones_sb = sb("ones_sb", [P, P])
        eps_sb = sb("eps_sb", [P, 1])
        mask_sb = sb("mask_sb", [P, CHUNK_TILES, SPAN])
        wsi_sb = sb("wsi_sb", [P, CHUNK_TILES, PROJ])
        mean_sb = sb("mean_sb", [P, 16])
        mean9 = sb("mean9", [P, 16])
        pat = sb("pat", [P, CHUNK_TILES, SPAN, PROJ])
        ws2 = sb("ws2", [P, E_DIM])
        gs_sb = sb("gs_sb", [D_SPARSE, E_DIM])
        ws_st = sb("ws_st", [P, E_DIM])
        ws_e = sb("ws_e", [P, P])
        gram = sb("gram", [P, P])
        wd_sb = sb("wd_sb", [P, D_CH, E_DIM])
        dense_sb = sb("dense_sb", [P, D_CH, BATCH])
        x_sq = sb("x_sq", [P, 512])
        x_std = sb("x_std", [P, 512])
        x_inv = sb("x_inv", [P, 512])
        x_t = sb("x_t", [P, BATCH])
        x_sum = sb("x_sum", [P, BATCH])
        gd_sb = sb("gd_sb", [P, 1])
        bd_sb = sb("bd_sb", [P, 1])
        u_sb = [sb(f"u_sb{h}", [P, UNIT, PROJ]) for h in range(2)]
        y_sq = sb("y_sq", [P, UNIT, PROJ])
        y_sum = sb("y_sum", [P, UNIT])
        y_std = sb("y_std", [P, UNIT])
        y_inv = sb("y_inv", [P, UNIT])
        items = [sb(f"items{h}", [P, UNIT, ITEMS]) for h in range(2)]
        pairs = [sb(f"pairs{h}", [P, ITEMS, BLK // 4]) for h in range(2)]
        packed = sb("packed", [P, STEPS, BODY])
        w9_sb = sb("w9_sb", [P, STEPS, MAXD])
        ga_sb = sb("ga_sb", [P, STEPS])
        gb_sb = sb("gb_sb", [P, STEPS])
        fac = sb("fac", [P, STEPS])
        bcols = sb("bcols", [P, 2])
        bq_sb = sb("bq_sb", [P, 8])
        selr_sb = sb("selr_sb", [P, PROJ])
        selc_sb = sb("selc_sb", [P, 8, PROJ])
        sel_a = sb("sel_a", [P, 8, PROJ])
        sel_b = sb("sel_b", [P, 8, PROJ])
        cs_sb = sb("cs_sb", [P, MAXD])
        o_sq = sb("o_sq", [P, O_CH, BODY])
        o_sb = sb("o_sb", [P, Z_CH, BODY])
        o_std = sb("o_std", [P, BODY])
        o_inv = sb("o_inv", [P, BODY])
        z_sb = sb("z_sb", [P, Z_CH, BODY])
        gl_sb = sb("gl_sb", [P, Z_CH])
        bl_sb = sb("bl_sb", [P, Z_CH])
        w1_sb = sb("w1_sb", [P, 6, H1])
        b1_sb = sb("b1_sb", [P, 4])
        b1f = sb("b1f", [P, 4])
        w2_sb = sb("w2_sb", [P, 4, H2])
        b2_sb = sb("b2_sb", [P, H2_CH])
        w3_sb = sb("w3_sb", [P, H2_CH])
        h1_sb = sb("h1_sb", [P, 4, BODY])
        h2_sb = sb("h2_sb", [P, H2_CH, BODY])
        y_out = sb("y_out", [1, BATCH])

        front_ps = ps("front_ps", [P, 512])
        u_ps = ps("u_ps", [P, 2, 512])
        y_ps = ps("y_ps", [P, 2, 512])
        z_ps = ps("z_ps", [P, 512])
        head_ps = ps("head_ps", [P, 4, BODY])

        w_in = [sem(f"w_in{n}") for n in range(6)]
        dense_in = [sem(f"dense_in{c}") for c in range(4)]
        ids_ready = sem("ids_ready")
        idx_copied = sem("idx_copied")
        gathered = [[sem(f"gath{h}{v}") for v in range(4)] for h in range(2)]
        prep = sem("prep")
        zeroed = sem("zeroed")
        prep_pe = sem("prep_pe")
        x_pe = sem("x_pe")
        x_sqd = sem("x_sqd")
        x_var = sem("x_var")
        x_stdd = sem("x_stdd")
        x_invd = sem("x_invd")
        x_nrm = sem("x_nrm")
        x_done = sem("x_done")
        xs_pe = sem("xs_pe")
        xs_done = sem("xs_done")
        turned = sem("turned")
        turned_sb = sem("turned_sb")
        gram_done = sem("gram_done")
        gram_prod = sem("gram_prod")
        gram_sum = sem("gram_sum")
        row_stdd = sem("row_stdd")
        row_invd = sem("row_invd")
        rows_scaled = sem("rows_scaled")
        u_done = sem("u_done")
        u_copied = sem("u_copied")
        y_done = sem("y_done")
        y_squared = sem("y_squared")
        y_summed = sem("y_summed")
        y_stdd = sem("y_stdd")
        y_invd = sem("y_invd")
        x_put = sem("x_put")
        items_done = sem("items_done")
        z_done = sem("z_done")
        pairs_done = sem("pairs_done")
        repacked = [sem(f"repacked{h}") for h in range(2)]
        sum_put = sem("sum_put")
        o_done = sem("o_done")
        o_squared = sem("o_squared")
        o_copied = sem("o_copied")
        ov_done = sem("ov_done")
        o_stdd = sem("o_stdd")
        o_invd = sem("o_invd")
        zn_done = sem("zn_done")
        h1_done = sem("h1_done")
        h1_relu = sem("h1_relu")
        h2_done = sem("h2_done")
        h2_relu = sem("h2_relu")
        yo_done = sem("yo_done")
        yo_copied = sem("yo_copied")
        stored = sem("stored")

        def wait(eng, s, value):
            if not isinstance(value, int) or value > 0:
                eng.wait_ge(s, value)

        block = ctx.enter_context(nc.Block())

        def passes(eng, body):
            body(0, True, False)
            with eng.Fori(1, PASSES - 1) as i:
                body(i, False, False)
            body(PASSES - 1, False, True)

        @block.sync
        def _(sp):
            def load(s, dst, src):
                sp.dma_start(dst, src).then_inc(s, 16)

            load(w_in[0], ids_raw[:], ids)
            load(w_in[0], size_sb[:], size_c)
            load(w_in[0], base_sb[:], base_c)
            load(w_in[1], ws2[:], wst2)
            load(w_in[1], eye_sb[:], eye)
            load(w_in[1], gs_sb[:], gs_b)
            load(w_in[1], mask_sb[:], mask13)
            load(w_in[1], wsi_sb[:], wsi13)
            sp.wait_ge(zeroed, 1)
            load(w_in[2], ws_st[D_SPARSE:D_SPARSE + 1, :], bs_row)
            load(w_in[2], wd_sb[:], wdt)
            load(w_in[2], gd_sb[:], gd_c)
            load(w_in[2], bd_sb[:], bd_c)
            for c in range(4):
                load(dense_in[c], dense_sb[:, :, c * 512:(c + 1) * 512], dense[:, :, c * 512:(c + 1) * 512])
            load(w_in[3], w9_sb[:], w9)
            load(w_in[3], ga_sb[:], ga)
            load(w_in[3], gb_sb[:], gb)
            load(w_in[3], bcols[:], bsi_cols)
            load(w_in[3], bq_sb[:], bsi_bq)
            load(w_in[3], selr_sb[:], sel_row)
            load(w_in[3], selc_sb[:], sel_col)
            load(w_in[4], w1_sb[:], w1)
            load(w_in[4], gl_sb[:], gl_c)
            load(w_in[4], bl_sb[:], bl_c)
            load(w_in[4], b1_sb[:], b1_c)
            load(w_in[5], w2_sb[:], w2)
            load(w_in[5], b2_sb[:], b2_c)
            load(w_in[5], w3_sb[:], w3)

            def repack(i, h):
                wait(sp, repacked[h], i * PACK_DMAS * 16)
                wait(sp, pairs_done, 8 * i + 4 * h + 4)
                if h == 0:
                    wait(sp, o_done, i)
                for j in range(4):
                    src = pairs[h][32 * j:32 * j + 32]
                    at = h * BLK + 32 * j
                    for qq in range(4):
                        sp.dma_start(packed[32 * qq:32 * qq + 32, 0:8, at:at + 32],
                                     src[:, 1 + 8 * qq:9 + 8 * qq, :]).then_inc(repacked[h], 16)
                    sp.dma_start(packed[0:32, 8, at:at + 32], src[:, 0, :]).then_inc(repacked[h], 16)
                    sp.dma_start(packed[32:64, 8, at:at + 32], src[:, ITEMS - 1, :]).then_inc(repacked[h], 16)

            def body(i, first, last):
                if not first:
                    repack(i - 1, 1)
                repack(i, 0)

            sp.wait_ge(zeroed, 2)
            passes(sp, body)
            repack(PASSES - 1, 1)
            sp.wait_ge(yo_copied, PASSES)
            sp.dma_start(out, y_out[:]).then_inc(stored, 16)
            sp.wait_ge(stored, 16)

        @block.gpsimd
        def _(pool):
            def gather(i, h):
                wait(pool, rows_scaled, 8 * i + 4 * h - 4)
                pool.tensor_copy(idx[h][:], idx_all[:, bass.ds((2 * i + h) * TILES, TILES)]).then_inc(idx_copied, 1)
                pool.wait_ge(idx_copied, 2 * i + h + 1)
                pool.nop(nofuse=True)
                for v, (lo, hi) in enumerate(GROUPS):
                    for t in range(lo, hi):
                        pool.indirect_dma_start(
                            rows[h][:, t, :], None, table,
                            bass.IndirectOffsetOnAxis(ap=idx[h][:, t:t + 1], axis=0)).then_inc(gathered[h][v], 16)

            def body(i, first, last):
                gather(i, 0)
                gather(i, 1)

            pool.wait_ge(ids_ready, 7)
            passes(pool, body)

        @block.tensor
        def _(pe):
            def transposes(q, k_par, v):
                lo, hi = GROUPS[v]
                n = (hi - lo) // 2
                wait(pe, gram_prod, q)
                for m in range(n):
                    src = rows[k_par][:, lo + 2 * m:lo + 2 * m + 2, :].rearrange("p a d -> p (a d)")
                    ins = nc.tensor.transpose(front_ps[:, m * P:(m + 1) * P], src, eye_sb[:])
                ins.then_inc(turned, 1)

            def gram_mm(q, v):
                lo, hi = GROUPS[v]
                pe.wait_ge(turned_sb, q + 1)
                for m in range((hi - lo) // 2):
                    ins = nc.tensor.matmul(front_ps[:, m * P:(m + 1) * P], rows_t[:, m * P:(m + 1) * P], gram[:],
                                           start=True, stop=True)
                ins.then_inc(gram_done, 1)

            def u_mm(u, k_par, v):
                pe.wait_ge(rows_scaled, u + 1)
                wait(pe, u_copied, u)
                ch, w = v // 2, v % 2
                for x in range(UNIT // BANK_B):
                    b0 = w * UNIT + x * BANK_B
                    fresh = True
                    for t in range(CHUNK_TILES):
                        lo, hi = max(tile_first(t), b0), min(tile_last(t) + 1, b0 + BANK_B)
                        if lo >= hi:
                            continue
                        ins = nc.tensor.matmul(
                            u_ps[0:D_SPARSE, x, (lo - b0) * PROJ:(hi - b0) * PROJ],
                            rows_n[k_par][:, ch * CHUNK_TILES + t, :],
                            pat[:, t, lo - tile_first(t):hi - tile_first(t), :].rearrange("p s q -> p (s q)"),
                            start=fresh, stop=True, skip_group_check=True)
                        fresh = False
                ins.then_inc(u_done, 1)

            def y_mm(u, par):
                pe.wait_ge(u_copied, u + 1)
                wait(pe, items_done, u)
                for x in range(UNIT // BANK_B):
                    ins = nc.tensor.matmul(y_ps[:, x, :], ws_st[:],
                                           u_sb[par][:, x * BANK_B:(x + 1) * BANK_B, :].rearrange("p b q -> p (b q)"),
                                           start=True, stop=True)
                ins.then_inc(y_done, 1)

            def z_mm(u, par):
                pe.wait_ge(items_done, u + 1)
                pe.wait_ge(x_put, u + 1)
                wait(pe, pairs_done, u)
                for g in range(GSLOTS):
                    for j in range(4):
                        t = items[par][:, j * GSLOTS + g, :]
                        ins = nc.tensor.matmul(z_ps[32 * j:32 * j + 32, g * ITEMS:(g + 1) * ITEMS],
                                               t[:, 1:1 + PROJ], t, start=True, stop=True)
                ins.then_inc(z_done, 1)

            def o_mm(i, cs):
                if cs[0] == 0:
                    for h in range(2):
                        pe.wait_ge(repacked[h], (i + 1) * PACK_DMAS * 16)
                    pe.wait_ge(sum_put, i + 1)
                    wait(pe, yo_copied, i)
                for c in cs:
                    for st in range(STEPS):
                        ins = nc.tensor.matmul(head_ps[:, c, :], w9_sb[:, st, c * P:(c + 1) * P], packed[:, st, :],
                                               start=(st == 0), stop=(st == STEPS - 1))
                if cs[-1] == O_CH - 1:
                    ins.then_inc(o_done, 1)

            def ov_mm(i):
                pe.wait_ge(o_squared, i + 1)
                pe.wait_ge(o_copied, i + 1)
                for c in range(O_CH):
                    ins = nc.tensor.matmul(head_ps[:, 0, :], ones_sb[:], o_sq[:, c, :],
                                           start=(c == 0), stop=(c == O_CH - 1))
                ins.then_inc(ov_done, 1)

            def h1_mm(i, cs):
                if cs[0] == 0:
                    pe.wait_ge(zn_done, i + 1)
                for c in cs:
                    for m in range(Z_CH):
                        nc.tensor.matmul(head_ps[:, c, :], w1_sb[:, m, c * P:(c + 1) * P], z_sb[:, m, :],
                                         start=(m == 0), stop=False)
                    for m in range(D_CH):
                        ins = nc.tensor.matmul(head_ps[:, c, :], w1_sb[:, 4 + m, c * P:(c + 1) * P],
                                               dense_sb[:, m, bass.ds(i * BODY, BODY)],
                                               start=False, stop=(m == D_CH - 1))
                ins.then_inc(h1_done, 1)

            def h2_mm(i):
                pe.wait_ge(h1_relu, 2 * i + 2)
                for c in range(H2_CH):
                    for m in range(4):
                        ins = nc.tensor.matmul(head_ps[:, c, :], w2_sb[:, m, c * P:(c + 1) * P], h1_sb[:, m, :],
                                               start=(m == 0), stop=(m == 3))
                ins.then_inc(h2_done, 1)

            def yo_mm(i):
                pe.wait_ge(h2_relu, i + 1)
                for m in range(H2_CH):
                    ins = nc.tensor.matmul(head_ps[0:1, 2, :], w3_sb[:, m:m + 1], h2_sb[:, m, :],
                                           start=(m == 0), stop=(m == H2_CH - 1))
                ins.then_inc(yo_done, 1)

            def head_slot(i, s):
                if s in (2, 3):
                    o_mm(i, (0, 1) if s == 2 else (2, 3))
                elif s == 4:
                    ov_mm(i)
                elif s in (5, 6):
                    h1_mm(i, (0, 1) if s == 5 else (2, 3))
                elif s == 7:
                    h2_mm(i)

            def body(i, first, last):
                for s in range(SLOTS):
                    u, k_par, v = 8 * i + s, s // 4, s % 4
                    nxt = not (last and s >= 4)
                    if not (last and s == SLOTS - 1):
                        u_mm(u + 1, ((s + 1) // 4) % 2, (v + 1) % 4)
                    if nxt:
                        wait(pe, gathered[1 - k_par][v],
                             (i + (1 if k_par == 0 else 2)) * 16 * (GROUPS[v][1] - GROUPS[v][0]))
                        transposes(u + 4, 1 - k_par, v)
                    if not first:
                        head_slot(i - 1, s)
                    if nxt:
                        gram_mm(u + 4, v)
                    if not (first and s == 0):
                        z_mm(u - 1, 1 - s % 2)
                    y_mm(u, s % 2)
                    if s == 7 and not first:
                        yo_mm(i - 1)

            pe.wait_ge(w_in[1], 5 * 16)
            pe.wait_ge(prep, 2)
            nc.tensor.transpose(y_ps[:, 0, 0:P], ws2[:], eye_sb[:]).then_inc(prep_pe, 1)
            pe.wait_ge(prep, 3)
            nc.tensor.matmul(y_ps[:, 1, 0:P], ws_e[:], ws_e[:], start=True, stop=True).then_inc(prep_pe, 1)
            pe.wait_ge(prep, 5)
            nc.tensor.matmul(u_ps[D_SPARSE:D_SPARSE + 1, 0, 0:PROJ], ones_sb[0:N_SPARSE, 0:1],
                             wsi_sb[0:N_SPARSE, 0, :], start=True, stop=True).then_inc(prep_pe, 1)

            pe.wait_ge(prep, 9)
            for c in range(4):
                pe.wait_ge(dense_in[c], 16)
                wait(pe, x_nrm, c)
                for m in range(D_CH):
                    ins = nc.tensor.matmul(y_ps[:, 0, :], wd_sb[:, m, :], dense_sb[:, m, c * 512:(c + 1) * 512],
                                           start=(m == 0), stop=(m == D_CH - 1))
                ins.then_inc(x_pe, 1)
                pe.wait_ge(x_sqd, c + 1)
                wait(pe, x_stdd, c)
                nc.tensor.matmul(y_ps[:, 1, :], ones_sb[:], x_sq[:], start=True, stop=True).then_inc(x_var, 1)
                pe.wait_ge(x_done, c + 1)
                wait(pe, xs_done, c)
                nc.tensor.matmul(u_ps[D_SPARSE:D_SPARSE + 1, 1, :], ones_sb[:, 0:1], x_t[:, c * 512:(c + 1) * 512],
                                 start=True, stop=True).then_inc(xs_pe, 1)

            for v in range(4):
                pe.wait_ge(gathered[0][v], 16 * (GROUPS[v][1] - GROUPS[v][0]))
                transposes(v, 0, v)
                if v == 0:
                    pe.wait_ge(prep, 4)
                gram_mm(v, v)
            pe.wait_ge(prep, 7)
            pe.wait_ge(xs_done, 4)
            u_mm(0, 0, 0)

            pe.wait_ge(prep, 12)
            for st in range(8):
                ins = nc.tensor.matmul(head_ps[32:64, 0:2, :].rearrange("p a n -> p (a n)"), sel_b[:, st, :],
                                       w9_sb[:, st, :], start=(st == 0), stop=(st == 7))
            ins.then_inc(prep_pe, 1)
            nc.tensor.matmul(head_ps[64:65, 2:4, :].rearrange("p a n -> p (a n)"), bcols[0:32, 0:1],
                             w9_sb[0:32, 8, :], start=True, stop=True).then_inc(prep_pe, 1)
            pe.wait_ge(prep, 14)
            nc.tensor.matmul(head_ps[96:97, 0:2, :].rearrange("p a n -> p (a n)"), bcols[32:64, 0:1],
                             cs_sb[32:64, :], start=True, stop=True).then_inc(prep_pe, 1)
            pe.wait_ge(w_in[4], 4 * 16)
            pe.wait_ge(prep, 16)
            for c in range(4):
                for m in range(Z_CH):
                    ins = nc.tensor.matmul(head_ps[:, 0, c:c + 1], w1_sb[:, m, c * P:(c + 1) * P], bl_sb[:, m:m + 1],
                                           start=(m == 0), stop=(m == Z_CH - 1))
            ins.then_inc(prep_pe, 1)
            pe.wait_ge(prep, 18)
            pe.wait_ge(w_in[5], 3 * 16)

            passes(pe, body)
            z_mm(UNITS * BLOCKS - 1, 1)
            for s in range(2, 8):
                head_slot(PASSES - 1, s)
            yo_mm(PASSES - 1)

        @block.scalar
        def _(act):
            def turn_copy(q, v):
                n = (GROUPS[v][1] - GROUPS[v][0]) // 2 * P
                act.wait_ge(turned, q + 1)
                wait(act, gram_done, q)
                nc.scalar.activation(rows_t[:, 0:n], front_ps[:, 0:n], ACT.Copy).then_inc(turned_sb, 1)

            def row_std_f(q, v):
                n = GROUPS[v][1] - GROUPS[v][0]
                act.wait_ge(gram_sum, q + 1)
                wait(act, row_invd, q)
                nc.scalar.activation(row_std[:, 0:n], row_var[:, 0:n], ACT.Sqrt, bias=eps_sb[:],
                                     scale=1.0 / E_DIM).then_inc(row_stdd, 1)

            def u_copy(u, par):
                act.wait_ge(u_done, u + 1)
                wait(act, y_done, u - 1)
                nc.scalar.activation(u_sb[par][0:D_SPARSE].rearrange("p b q -> p (b q)"),
                                     u_ps[0:D_SPARSE].rearrange("p a n -> p (a n)"), ACT.Copy).then_inc(u_copied, 1)

            def y_square(u):
                act.wait_ge(y_done, u + 1)
                wait(act, y_summed, u)
                nc.scalar.activation(y_sq[:].rearrange("p b q -> p (b q)"),
                                     y_ps[:].rearrange("p a n -> p (a n)"), ACT.Square).then_inc(y_squared, 1)

            def y_std_f(u):
                act.wait_ge(y_summed, u + 1)
                wait(act, y_invd, u)
                nc.scalar.activation(y_std[:], y_sum[:], ACT.Sqrt, bias=eps_sb[:],
                                     scale=1.0 / PROJ).then_inc(y_stdd, 1)

            def z_copy(u, k_par, v, before):
                act.wait_ge(z_done, u + 1)
                if v == 0:
                    wait(act, repacked[k_par], before * PACK_DMAS * 16)
                nc.scalar.activation(
                    pairs[k_par][:, :, v * GSLOTS:(v + 1) * GSLOTS].rearrange("p q g -> p g q"),
                    z_ps[:, 0:GSLOTS * ITEMS].rearrange("p (g q) -> p g q", q=ITEMS),
                    ACT.Copy).then_inc(pairs_done, 1)

            def head_slot(i, s):
                if s == 3:
                    act.wait_ge(o_done, i + 1)
                    nc.scalar.activation(o_sq[:].rearrange("p c n -> p (c n)"),
                                         head_ps[:].rearrange("p c n -> p (c n)"), ACT.Square).then_inc(o_squared, 1)
                elif s == 4:
                    act.wait_ge(ov_done, i + 1)
                    nc.scalar.activation(o_std[:], head_ps[:, 0, :], ACT.Sqrt, bias=eps_sb[:],
                                         scale=1.0 / MAXD).then_inc(o_stdd, 1)
                elif s in (5, 6):
                    act.wait_ge(h1_done, 2 * i + s - 4)
                    for c in ((0, 1) if s == 5 else (2, 3)):
                        ins = nc.scalar.activation(h1_sb[:, c, :], head_ps[:, c, :], ACT.Relu, bias=b1f[:, c:c + 1])
                    ins.then_inc(h1_relu, 1)
                elif s == 7:
                    act.wait_ge(h2_done, i + 1)
                    for c in range(H2_CH):
                        ins = nc.scalar.activation(h2_sb[:, c, :], head_ps[:, c, :], ACT.Relu, bias=b2_sb[:, c:c + 1])
                    ins.then_inc(h2_relu, 1)

            def yo_copy(i):
                act.wait_ge(yo_done, i + 1)
                nc.scalar.activation(y_out[:, bass.ds(i * BODY, BODY)], head_ps[0:1, 2, :],
                                     ACT.Copy).then_inc(yo_copied, 1)

            def body(i, first, last):
                for s in range(SLOTS):
                    u, k_par, v = 8 * i + s, s // 4, s % 4
                    nxt = not (last and s >= 4)
                    if not (last and s == SLOTS - 1):
                        u_copy(u + 1, 1 - s % 2)
                    if not (first and s == 0):
                        y_std_f(u - 1)
                    if nxt:
                        turn_copy(u + 4, v)
                    if not first:
                        head_slot(i - 1, s)
                    if nxt:
                        row_std_f(u + 4, v)
                    if not (first and s == 0):
                        pk, pv = ((s - 1) // 4) % 2, (s - 1) % 4
                        z_copy(u - 1, pk, pv, i)
                    y_square(u)
                    if s == 7 and not first:
                        yo_copy(i - 1)

            act.wait_ge(zeroed, 3)
            for c in range(4):
                act.wait_ge(x_pe, c + 1)
                wait(act, x_var, c)
                nc.scalar.activation(x_sq[:], y_ps[:, 0, :], ACT.Square).then_inc(x_sqd, 1)
                act.wait_ge(x_var, c + 1)
                wait(act, x_invd, c)
                nc.scalar.activation(x_std[:], y_ps[:, 1, :], ACT.Sqrt, bias=eps_sb[:],
                                     scale=1.0 / E_DIM).then_inc(x_stdd, 1)
                act.wait_ge(xs_pe, c + 1)
                nc.scalar.activation(x_sum[D_SPARSE:D_SPARSE + 1, c * 512:(c + 1) * 512],
                                     u_ps[D_SPARSE:D_SPARSE + 1, 1, :], ACT.Copy).then_inc(xs_done, 1)
            for v in range(4):
                turn_copy(v, v)
                row_std_f(v, v)
            u_copy(0, 0)
            act.wait_ge(prep, 18)
            act.wait_ge(w_in[5], 3 * 16)
            passes(act, body)
            y_std_f(UNITS * BLOCKS - 1)
            z_copy(UNITS * BLOCKS - 1, 1, 3, PASSES)
            for s in range(3, 8):
                head_slot(PASSES - 1, s)
            yo_copy(PASSES - 1)

        @block.vector
        def _(dve):
            V = nc.vector

            def gram_reduce(q, k_par, v):
                lo, hi = GROUPS[v]
                n = hi - lo
                pr = prod[:, 0:n * D_SPARSE].rearrange("p (t d) -> p t d", d=D_SPARSE)
                dve.wait_ge(gram_done, q + 1)
                V.tensor_tensor(pr, front_ps[:, 0:n * D_SPARSE].rearrange("p (t d) -> p t d", d=D_SPARSE),
                                rows[k_par][:, lo:hi, :], ALU.mult).then_inc(gram_prod, 1)
                dve.wait_ge(gram_prod, q + 1)
                V.tensor_reduce(out=row_var[:, 0:n], in_=pr, axis=AX, op=ALU.add).then_inc(gram_sum, 1)

            def scale_rows(q, k_par, v):
                lo, hi = GROUPS[v]
                n = hi - lo
                dve.wait_ge(row_stdd, q + 1)
                V.reciprocal(row_inv[:, 0:n], row_std[:, 0:n]).then_inc(row_invd, 1)
                dve.wait_ge(row_invd, q + 1)
                wait(dve, u_done, q - v - 4)
                V.tensor_tensor(rows_n[k_par][:, lo:hi, :], rows[k_par][:, lo:hi, :],
                                row_inv[:, 0:n].unsqueeze(2).to_broadcast([P, n, D_SPARSE]),
                                ALU.mult).then_inc(rows_scaled, 1)

            def y_reduce(u):
                dve.wait_ge(y_squared, u + 1)
                wait(dve, y_stdd, u)
                V.tensor_reduce(out=y_sum[:], in_=y_sq[:], axis=AX, op=ALU.add).then_inc(y_summed, 1)

            def put_x(u, par, k, v):
                wait(dve, z_done, u - 1)
                src = x_t[:, bass.ds(k * BLK, BLK)].rearrange("p (j v g) -> p v j g", j=4, v=4)[:, v]
                V.tensor_copy(items[par][:, :, 0].rearrange("p (j g) -> p j g", j=4), src).then_inc(x_put, 1)

            def normalise(u, par):
                dve.wait_ge(y_stdd, u + 1)
                V.reciprocal(y_inv[:], y_std[:]).then_inc(y_invd, 1)
                dve.wait_ge(y_invd, u + 1)
                wait(dve, z_done, u - 1)
                V.tensor_tensor(items[par][:, :, 1:1 + PROJ], y_ps[:].rearrange("p a (b q) -> p (a b) q", q=PROJ),
                                y_inv[:].unsqueeze(2).to_broadcast([P, UNIT, PROJ]), ALU.mult).then_inc(items_done, 1)

            def head_slot(i, s):
                if s == 1:
                    wait(dve, o_done, i)
                    V.tensor_copy(packed[64:65, 8, :], x_sum[64:65, bass.ds(i * BODY, BODY)]).then_inc(sum_put, 1)
                elif s == 3:
                    dve.wait_ge(o_squared, i + 1)
                    V.tensor_copy(o_sb[:].rearrange("p c n -> p (c n)"),
                                  head_ps[:, 0:Z_CH, :].rearrange("p c n -> p (c n)")).then_inc(o_copied, 1)
                elif s == 4:
                    dve.wait_ge(o_stdd, i + 1)
                    V.reciprocal(o_inv[:], o_std[:]).then_inc(o_invd, 1)
                    dve.wait_ge(o_invd, i + 1)
                    wait(dve, h1_done, 2 * i)
                    V.tensor_tensor(z_sb[:], o_sb[:], o_inv[:].unsqueeze(1).to_broadcast([P, Z_CH, BODY]),
                                    ALU.mult).then_inc(zn_done, 1)

            def body(i, first, last):
                for s in range(SLOTS):
                    u, k_par, v = 8 * i + s, s // 4, s % 4
                    nxt = not (last and s >= 4)
                    if not (first and s == 0):
                        normalise(u - 1, 1 - s % 2)
                    put_x(u, s % 2, 2 * i + k_par, v)
                    if not first:
                        head_slot(i - 1, s)
                    if nxt:
                        gram_reduce(u + 4, 1 - k_par, v)
                        scale_rows(u + 4, 1 - k_par, v)
                    y_reduce(u)

            V.memset(ws_st[64:128, :], 0.0).then_inc(zeroed, 1)
            V.memset(packed[64:128, 8, :], 0.0).then_inc(zeroed, 1)
            V.memset(eps_sb[:], EPS).then_inc(zeroed, 1)
            V.memset(u_sb[0][64:128], 0.0).then_inc(zeroed, 1)
            V.memset(u_sb[1][64:128], 0.0).then_inc(zeroed, 1)
            V.memset(ones_sb[:], 1.0).then_inc(zeroed, 1)
            V.memset(gram[:], 0.0).then_inc(zeroed, 1)
            V.memset(items[0][:, :, ITEMS - 1], 1.0).then_inc(zeroed, 1)
            V.memset(items[1][:, :, ITEMS - 1], 1.0).then_inc(zeroed, 1)
            dve.wait_ge(zeroed, 9)
            V.memset(packed[96:97, 8, :], 1.0).then_inc(zeroed, 1)

            dve.wait_ge(w_in[0], 3 * 16)
            three = [P, BLOCKS * 2, CHUNK_TILES]

            def by_tile(t):
                return t[:].rearrange("p (c t) -> p c t", t=CHUNK_TILES)

            def const(t):
                return t[:].unsqueeze(1).to_broadcast(three)

            V.tensor_scalar(last_sb[:], size_sb[:], -1.0, None, ALU.add).then_inc(ids_ready, 1)
            V.tensor_scalar(ids_f[:], ids_raw[:], 0.0, None, ALU.is_lt).then_inc(ids_ready, 1)
            dve.wait_ge(ids_ready, 2)
            V.tensor_tensor(by_tile(ids_g), by_tile(ids_f), const(size_sb), ALU.mult).then_inc(ids_ready, 1)
            dve.wait_ge(ids_ready, 3)
            V.tensor_tensor(ids_f[:], ids_raw[:], ids_g[:], ALU.add).then_inc(ids_ready, 1)
            dve.wait_ge(ids_ready, 4)
            V.tensor_scalar(ids_g[:], ids_f[:], 0.0, None, ALU.max).then_inc(ids_ready, 1)
            dve.wait_ge(ids_ready, 5)
            V.tensor_tensor(by_tile(ids_f), by_tile(ids_g), const(last_sb), ALU.min).then_inc(ids_ready, 1)
            dve.wait_ge(ids_ready, 6)
            V.tensor_tensor(by_tile(idx_all), by_tile(ids_f), const(base_sb), ALU.add).then_inc(ids_ready, 1)

            dve.wait_ge(w_in[1], 5 * 16)
            V.tensor_reduce(out=mean_sb[:, 0:1], in_=ws2[:], axis=AX, op=ALU.add).then_inc(zeroed, 1)
            dve.wait_ge(zeroed, 11)
            V.tensor_scalar(mean_sb[:, 0:1], mean_sb[:, 0:1], 1.0 / E_DIM, None, ALU.mult).then_inc(prep, 1)
            dve.wait_ge(prep, 1)
            V.tensor_scalar(ws2[:], ws2[:], mean_sb[:, 0:1], None, ALU.subtract).then_inc(prep, 1)
            dve.wait_ge(prep_pe, 1)
            V.tensor_copy(ws_e[:], y_ps[:, 0, 0:P]).then_inc(prep, 1)
            dve.wait_ge(prep_pe, 2)
            V.tensor_copy(gram[0:64, 0:64], y_ps[0:64, 1, 0:64]).then_inc(zeroed, 1)
            dve.wait_ge(zeroed, 12)
            V.tensor_copy(gram[64:128, 64:128], y_ps[64:128, 1, 64:128]).then_inc(prep, 1)

            V.tensor_reduce(out=mean_sb[:, 1:1 + CHUNK_TILES], in_=wsi_sb[:], axis=AX, op=ALU.add).then_inc(zeroed, 1)
            dve.wait_ge(zeroed, 13)
            V.tensor_scalar(mean_sb[:, 1:1 + CHUNK_TILES], mean_sb[:, 1:1 + CHUNK_TILES], 1.0 / PROJ, None,
                            ALU.mult).then_inc(zeroed, 1)
            dve.wait_ge(zeroed, 14)
            V.tensor_tensor(wsi_sb[:], wsi_sb[:], mean_sb[:, 1:1 + CHUNK_TILES].unsqueeze(2).to_broadcast(
                [P, CHUNK_TILES, PROJ]), ALU.subtract).then_inc(prep, 1)
            dve.wait_ge(prep, 5)
            V.tensor_tensor(pat[:], wsi_sb[:].unsqueeze(2).to_broadcast([P, CHUNK_TILES, SPAN, PROJ]),
                            mask_sb[:].unsqueeze(3).to_broadcast([P, CHUNK_TILES, SPAN, PROJ]),
                            ALU.mult).then_inc(prep, 1)
            dve.wait_ge(prep_pe, 3)
            for h in range(2):
                ins = V.tensor_copy(u_sb[h][64:65], u_ps[64:65, 0, 0:PROJ].unsqueeze(1).to_broadcast([1, UNIT, PROJ]))
            ins.then_inc(prep, 1)
            V.tensor_tensor(ws_st[0:64, :], ws2[0:64, :], gs_sb[:], ALU.mult).then_inc(prep, 1)

            dve.wait_ge(w_in[2], 4 * 16)
            V.tensor_reduce(out=mean9[:, 9:11], in_=wd_sb[:], axis=AX, op=ALU.add).then_inc(zeroed, 1)
            dve.wait_ge(zeroed, 15)
            V.tensor_scalar(mean9[:, 9:11], mean9[:, 9:11], 1.0 / E_DIM, None, ALU.mult).then_inc(zeroed, 1)
            dve.wait_ge(zeroed, 16)
            V.tensor_tensor(wd_sb[:], wd_sb[:], mean9[:, 9:11].unsqueeze(2).to_broadcast([P, D_CH, E_DIM]),
                            ALU.subtract).then_inc(prep, 1)
            for c in range(4):
                dve.wait_ge(x_stdd, c + 1)
                V.reciprocal(x_inv[:], x_std[:]).then_inc(x_invd, 1)
                dve.wait_ge(x_invd, c + 1)
                V.tensor_tensor(x_t[:, c * 512:(c + 1) * 512], y_ps[:, 0, :], x_inv[:], ALU.mult).then_inc(x_nrm, 1)
                dve.wait_ge(x_nrm, c + 1)
                V.tensor_scalar(x_t[:, c * 512:(c + 1) * 512], x_t[:, c * 512:(c + 1) * 512], gd_sb[:], bd_sb[:],
                                ALU.mult, ALU.add).then_inc(x_done, 1)
            for v in range(4):
                gram_reduce(v, 0, v)
                scale_rows(v, 0, v)

            dve.wait_ge(w_in[3], 7 * 16)
            V.tensor_reduce(out=mean9[:, 0:STEPS], in_=w9_sb[:], axis=AX, op=ALU.add).then_inc(zeroed, 1)
            V.tensor_tensor(fac[:], ga_sb[:], gb_sb[:], ALU.mult).then_inc(zeroed, 1)
            dve.wait_ge(zeroed, 18)
            V.tensor_scalar(mean9[:, 0:STEPS], mean9[:, 0:STEPS], 1.0 / MAXD, None, ALU.mult).then_inc(zeroed, 1)
            dve.wait_ge(zeroed, 19)
            V.tensor_tensor(w9_sb[:], w9_sb[:], mean9[:, 0:STEPS].unsqueeze(2).to_broadcast([P, STEPS, MAXD]),
                            ALU.subtract).then_inc(prep, 1)
            V.tensor_tensor(sel_a[:], selr_sb[:].unsqueeze(1).to_broadcast([P, 8, PROJ]),
                            bq_sb[:].unsqueeze(2).to_broadcast([P, 8, PROJ]), ALU.mult).then_inc(prep, 1)
            V.tensor_scalar(sel_b[:], selc_sb[:], bcols[:, 1:2], None, ALU.mult).then_inc(zeroed, 1)
            dve.wait_ge(prep, 11)
            dve.wait_ge(zeroed, 20)
            V.tensor_tensor(sel_b[:], sel_b[:], sel_a[:], ALU.add).then_inc(prep, 1)
            dve.wait_ge(prep_pe, 5)
            V.tensor_copy(cs_sb[32:64, :], head_ps[32:64, 0:2, :].rearrange("p a n -> p (a n)")).then_inc(prep, 1)
            V.tensor_tensor(w9_sb[:], w9_sb[:], fac[:].unsqueeze(2).to_broadcast([P, STEPS, MAXD]),
                            ALU.mult).then_inc(zeroed, 1)
            dve.wait_ge(zeroed, 21)
            dve.wait_ge(prep, 13)
            V.tensor_scalar(w9_sb[32:64, 8, :], cs_sb[32:64, :], ga_sb[32:64, 8:9], None, ALU.mult).then_inc(prep, 1)
            V.tensor_copy(w9_sb[64:65, 8, :], head_ps[64:65, 2:4, :].rearrange("p a n -> p (a n)")).then_inc(prep, 1)
            dve.wait_ge(prep_pe, 6)
            V.tensor_scalar(w9_sb[96:97, 8, :], head_ps[96:97, 0:2, :].rearrange("p a n -> p (a n)"),
                            float(E_DIM) / 2.0, None, ALU.mult).then_inc(prep, 1)
            dve.wait_ge(prep_pe, 7)
            V.tensor_tensor(b1f[:], head_ps[:, 0, 0:4], b1_sb[:], ALU.add).then_inc(prep, 1)
            V.tensor_tensor(w1_sb[:, 0:Z_CH, :], w1_sb[:, 0:Z_CH, :],
                            gl_sb[:].unsqueeze(2).to_broadcast([P, Z_CH, H1]), ALU.mult).then_inc(prep, 1)

            passes(dve, body)
            normalise(UNITS * BLOCKS - 1, 1)
            for s in (1, 3, 4):
                head_slot(PASSES - 1, s)




def kernel(**inputs):
    import numpy as np
    import concourse.bacc as bacc
    from concourse import mybir as _mybir
    from concourse.bass_utils import run_bass_kernel_spmd as run

    a = {k: np.asarray(v) for k, v in inputs.items()}
    f32 = np.float32
    tile_rows = np.arange(CHUNK * N_SPARSE).reshape(CHUNK_TILES, P).T
    of_table, of_sample = tile_rows % N_SPARSE, tile_rows // N_SPARSE
    sizes = np.array([a[f"tbl_{n}"].shape[0] for n in range(N_SPARSE)])
    firsts = np.concatenate([[0], np.cumsum(sizes)[:-1]])
    first_of = np.array([tile_first(t) for t in range(CHUNK_TILES)])
    mask = (of_sample - first_of)[:, :, None] == np.arange(SPAN)[None, None, :]

    part = np.arange(P)
    p_of, q_of = part[:, None] % PROJ, 8 * (part[:, None] // PROJ) + np.arange(8)[None, :]
    low = p_of > q_of
    pair = np.where(low, (p_of + 1) * p_of // 2 + q_of + 1, 0)
    wl_t = a["L0_rec_Wl"].T
    w9 = np.zeros((P, STEPS, MAXD), f32)
    w9[:, 0:8, :][low] = wl_t[pair[low]]
    one = np.arange(PROJ)
    w9[0:PROJ, 8, :] = wl_t[(one + 1) * one // 2]
    gsi, bsi = a["L0_rec_gsi"], a["L0_rec_bsi"]
    ga = np.ones((P, STEPS), f32)
    gb = np.ones((P, STEPS), f32)
    ga[:, 0:8] = gsi[np.broadcast_to(p_of, (P, 8))]
    gb[:, 0:8] = gsi[q_of]
    ga[:, 8] = gsi[part % PROJ]
    dense_t = a["r_dense_t"].T.reshape(D_CH, P, BLOCKS, UNITS, 4, GSLOTS).transpose(1, 0, 2, 4, 3, 5)
    w1 = a["W_top1"].reshape(6, P, H1).transpose(1, 0, 2)

    given = {
        "table": np.concatenate([a[f"tbl_{n}"] for n in range(N_SPARSE)], axis=0),
        "ids": a["ids"].reshape(BLOCKS * TILES, P).T,
        "dense": dense_t.reshape(P, D_CH, BATCH),
        "size_c": sizes[of_table].astype(f32),
        "base_c": firsts[of_table].astype(f32),
        "eye": np.eye(P, dtype=f32),
        "mask13": mask.astype(f32),
        "sel_row": (part[:, None] % PROJ == one[None, :]).astype(f32),
        "sel_col": (q_of[:, :, None] == one[None, None, :]).astype(f32),
        "wst2": np.concatenate([a["L0_rec_Ws"].T] * 2, axis=0),
        "gs_b": np.broadcast_to(a["L0_rec_gs"], (D_SPARSE, E_DIM)),
        "bs_row": a["L0_rec_bs"].reshape(1, E_DIM),
        "wdt": a["L0_rec_Wd"].T.reshape(D_CH, P, E_DIM).transpose(1, 0, 2),
        "gd_c": a["L0_rec_gd"].reshape(P, 1),
        "bd_c": a["L0_rec_bd"].reshape(P, 1),
        "wsi13": a["L0_rec_Wsi"].T[of_table],
        "w9": w9, "ga": ga, "gb": gb,
        "bsi_cols": np.stack([bsi[part % PROJ]] * 2, axis=1),
        "bsi_bq": bsi[q_of],
        "gl_c": a["L0_rec_gl"][0:DIMS_IN_USE].reshape(Z_CH, P).T,
        "bl_c": a["L0_rec_bl"][0:DIMS_IN_USE].reshape(Z_CH, P).T,
        "w1": w1,
        "b1_c": a["b_top1"].reshape(4, P).T,
        "w2": a["W_top2"].reshape(4, P, H2).transpose(1, 0, 2),
        "b2_c": a["b_top2"].reshape(H2_CH, P).T,
        "w3": a["W_top3"].reshape(H2_CH, P).T,
    }
    nc = bacc.Bacc("TRN2", target_bir_lowering=False, num_devices=1)
    arrays, args = {}, {}
    for name, v in given.items():
        v = np.ascontiguousarray(v)
        arrays[f"in_{name}"] = v
        args[name] = nc.dram_tensor(f"in_{name}", v.shape, _mybir.dt.from_np(v.dtype), kind="ExternalInput").ap()
    out = nc.dram_tensor("out_y", (1, BATCH), _mybir.dt.float32, kind="ExternalOutput").ap()
    build_program(nc, out=out, **args)
    r = run(nc, [arrays], core_ids=[0])
    y = r.results[0]["out_y"].reshape(BLOCKS, 4, UNITS, GSLOTS).transpose(0, 2, 1, 3)
    return y.reshape(BATCH, 1)
```

```python
from contextlib import ExitStack

import concourse.bass as bass
from concourse import mybir

BATCH = 2048
N_SPARSE = 26
D_SPARSE = 64
D_DENSE = 256
E_DIM = 128
PROJ = 32
N_FLAT = 528
MAXD = 512
DIMS_IN_USE = 384
H1, H2 = 512, 256
EPS = 1e-05

P = 128
BLK = 128
BLOCKS = BATCH // BLK
TILES = BLK * N_SPARSE // P
CHUNK = 64
CHUNK_TILES = CHUNK * N_SPARSE // P
UNIT = 32
UNITS = BLK // UNIT
BANK_B = 512 // PROJ
SPAN = -(-(P + N_SPARSE - 1) // N_SPARSE)
GROUPS = [(0, 8), (8, 14), (14, 20), (20, 26)]
ITEMS = PROJ + 2
GSLOTS = UNIT // 4
STEPS = 5
LAST = STEPS - 1
STRIPS = [(1, 0, 4, 0, 0), (5, 4, 4, 0, 31), (9, 8, 4, 0, 58), (13, 12, 4, 0, 81), (17, 16, 4, 0, 100),
          (21, 20, 4, 0, 115)]
STRIPS += [(25, 24 + n, 1, LAST, 65 + 7 * n) for n in range(4)] + [(29, 28 + n, 1, LAST, 97 + 3 * n) for n in range(4)]
ROW_SUM, ROW_ONE = 64, 96
BODY = 2 * BLK
PASSES = BATCH // BODY
SLOTS = BODY // UNIT
O_CH = MAXD // P
Z_CH = DIMS_IN_USE // P
D_CH = D_DENSE // P
X_CHUNK = 512
X_CHUNKS = BATCH // X_CHUNK
H2_CH = H2 // P
PACK_DMAS = len(STRIPS) + 2


def tile_first(t):
    return t * P // N_SPARSE


def tile_last(t):
    return (t * P + P - 1) // N_SPARSE


def build_program(nc, table, ids, dense, size_c, base_c, eye, mask13, sel_p, sel_q,
                  wst2, gs_b, bs_b, wdt, gd_c, bd_c, wsi13, wl, ga, gb, bsi_c, bsi_p, bsi_q, bs_pick,
                  gl_c, bl_c, w1, b1_c, w2, b2_c, w3, spill, out):
    fp32 = mybir.dt.float32
    f32r = mybir.dt.float32r
    i32 = mybir.dt.int32
    ALU = mybir.AluOpType
    ACT = mybir.ActivationFunctionType
    AX = mybir.AxisListType.X

    with ExitStack() as ctx:
        def sb(name, shape, dt=fp32):
            return ctx.enter_context(nc.sbuf_tensor(name, shape, dt))

        def ps(name, shape):
            return ctx.enter_context(nc.psum_tensor(name, shape, fp32))

        def sem(name):
            return ctx.enter_context(nc.semaphore(name))

        ids_raw = sb("ids_raw", [P, BLOCKS * TILES], i32)
        idx_all = sb("idx_all", [P, BLOCKS * TILES], i32)
        size_sb = sb("size_sb", [P, CHUNK_TILES])
        last_sb = sb("last_sb", [P, CHUNK_TILES])
        base_sb = sb("base_sb", [P, CHUNK_TILES])
        idx = [sb(f"idx{h}", [P, TILES], i32) for h in range(2)]
        rows = [sb(f"rows{h}", [P, TILES, D_SPARSE]) for h in range(2)]
        rows_f = sb("rows_f", [P, 8, D_SPARSE])
        rows_s = sb("rows_s", [P, TILES, 2, D_SPARSE], f32r)
        rows_t = sb("rows_t", [P, 4 * P])
        prod = sb("prod", [P, 8 * D_SPARSE])
        row_var = sb("row_var", [P, 8])
        row_std = sb("row_std", [P, 8])
        row_inv = sb("row_inv", [P, 8])
        eye_sb = sb("eye_sb", [P, P])
        ones_sb = sb("ones_sb", [P, P])
        eps_sb = sb("eps_sb", [P, 1])
        mask_sb = sb("mask_sb", [P, CHUNK_TILES, SPAN])
        wsi_sb = sb("wsi_sb", [P, CHUNK_TILES, PROJ])
        ws_mean = sb("ws_mean", [P, 1])
        wsi_mean = sb("wsi_mean", [P, CHUNK_TILES])
        wd_mean = sb("wd_mean", [P, D_CH])
        wl_mean = sb("wl_mean", [P, STEPS])
        wss_h = sb("wss_h", [P, PROJ], f32r)
        wss_l = sb("wss_l", [P, PROJ])
        pat_h = sb("pat_h", [P, CHUNK_TILES, SPAN, PROJ], f32r)
        pat_l = sb("pat_l", [P, CHUNK_TILES, SPAN, PROJ], f32r)
        ws2 = sb("ws2", [P, E_DIM])
        gs_sb = sb("gs_sb", [P, E_DIM])
        bs_sb = sb("bs_sb", [P, E_DIM])
        pick_sb = sb("pick_sb", [P, 2])
        ws_g = sb("ws_g", [P, E_DIM])
        ws_h = sb("ws_h", [P, E_DIM], f32r)
        ws_l = sb("ws_l", [P, E_DIM], f32r)
        ws_b = sb("ws_b", [P, E_DIM], f32r)
        bs_h = sb("bs_h", [P, E_DIM], f32r)
        bs_t = sb("bs_t", [P, E_DIM])
        bs_u = sb("bs_u", [P, E_DIM])
        ws_e = sb("ws_e", [P, P])
        gram = sb("gram", [P, P])
        wd_sb = sb("wd_sb", [P, D_CH, E_DIM])
        dense_mem = sb("dense_mem", [P, 2, D_CH * BODY])
        dense_sb = [dense_mem[:, h].rearrange("p (m n) -> p m n", m=D_CH) for h in range(2)]
        x_dense = dense_mem[:].rearrange("p h w -> p (h w)").rearrange("p (m n) -> p m n", m=D_CH)
        x_sq = prod[:]
        x_t = sb("x_t", [P, BATCH])
        lines = sb("lines", [P, BATCH])
        x_sum = lines[64:65, :]
        y_out = lines[0:1, :]
        gd_sb = sb("gd_sb", [P, 1])
        bd_sb = sb("bd_sb", [P, 1])
        u_h = [sb(f"u_h{h}", [P, UNIT, PROJ], f32r) for h in range(2)]
        u_l = [sb(f"u_l{h}", [P, UNIT, PROJ], f32r) for h in range(2)]
        y_sq = sb("y_sq", [P, UNIT, PROJ])
        y_sum = sb("y_sum", [P, UNIT])
        y_std = sb("y_std", [P, UNIT])
        y_inv = sb("y_inv", [P, UNIT])
        items = [sb(f"items{h}", [P, UNIT, ITEMS]) for h in range(2)]
        pair_words = ITEMS * BODY // 4
        pair_mem = sb("pair_mem", [P, 2 * pair_words])
        pairs = [pair_mem[:, h * pair_words:(h + 1) * pair_words].rearrange("p (q n) -> p q n", q=ITEMS)
                 for h in range(2)]
        pat_words = CHUNK_TILES * SPAN * PROJ
        pat = pair_mem[:, 0:pat_words].rearrange("p (t s q) -> p t s q", t=CHUNK_TILES, s=SPAN)
        ids_f, ids_g = [pair_mem[:, pat_words + h * BLOCKS * TILES:pat_words + (h + 1) * BLOCKS * TILES]
                        for h in range(2)]
        packed = sb("packed", [P, STEPS, BODY])
        packed_h = sb("packed_h", [P, STEPS, BODY], f32r)
        packed_l = sb("packed_l", [P, STEPS, BODY], f32r)
        x_var = sb("x_var", [P, X_CHUNK // P])
        x_std = sb("x_std", [P, X_CHUNK // P])
        x_inv = sb("x_inv", [P, X_CHUNK // P])
        wl_h = sb("wl_h", [P, STEPS, MAXD], f32r)
        wl_l = sb("wl_l", [P, STEPS, MAXD], f32r)
        ga_sb = sb("ga_sb", [P, STEPS])
        gb_sb = sb("gb_sb", [P, STEPS])
        fac = sb("fac", [P, STEPS])
        bc_sb = sb("bc_sb", [P, 1])
        bp_sb = sb("bp_sb", [P, STEPS])
        bq_sb = sb("bq_sb", [P, STEPS])
        sel_mem = sb("sel_mem", [P, 4, STEPS, PROJ])
        selp_sb, selq_sb, sel_a, sel_b = [sel_mem[:, n] for n in range(4)]
        cs_sb = lines
        o_mem = sb("o_mem", [P, 2, BODY])
        o_std, o_inv = o_mem[:, 0], o_mem[:, 1]
        x_rows = o_mem[:].rearrange("p h n -> p (h n)")
        head_mem = sb("head_mem", [P, (O_CH + 2 * Z_CH + 4 + H2_CH) * BODY])
        head_rows = head_mem[:].rearrange("p (c n) -> p c n", n=BODY)
        at = 0
        head_parts = []
        for n in (O_CH, Z_CH, Z_CH, 4, H2_CH):
            head_parts.append(head_rows[:, at:at + n, :])
            at += n
        o_sq, o_sb, z_sb, h1_sb, h2_sb = head_parts
        wl_sb = head_mem[:, 0:STEPS * MAXD].rearrange("p (s o) -> p s o", s=STEPS)
        gl_sb = sb("gl_sb", [P, Z_CH])
        bl_sb = sb("bl_sb", [P, Z_CH])
        w1_sb = sb("w1_sb", [P, Z_CH + D_CH, H1])
        b1_sb = sb("b1_sb", [P, 4])
        b1f = sb("b1f", [P, 4])
        w2_sb = sb("w2_sb", [P, 4, H2])
        b2_sb = sb("b2_sb", [P, H2_CH])
        w3_sb = sb("w3_sb", [P, H2_CH])

        front_ps = ps("front_ps", [P, 512])
        u_ps = ps("u_ps", [P, 2, 512])
        y_ps = ps("y_ps", [P, 2, 512])
        z_ps = ps("z_ps", [P, 512])
        head_ps = ps("head_ps", [P, 4, BODY])

        w_in = [sem(f"w_in{n}") for n in range(6)]
        dense_in = [sem(f"dense_in{c}") for c in range(4)]
        head_in = [sem(f"head_in{h}") for h in range(2)]
        ids_ready = sem("ids_ready")
        idx_copied = sem("idx_copied")
        gathered = [[sem(f"gath{h}{v}") for v in range(4)] for h in range(2)]
        zeroed = sem("zeroed")
        prep = sem("prep")
        prep_pe = sem("prep_pe")
        prep_act = sem("prep_act")
        sums = sem("sums")
        wl_sum = sem("wl_sum")
        wl_prep = sem("wl_prep")
        wl_pe = sem("wl_pe")
        wl_act = sem("wl_act")
        x_pe = sem("x_pe")
        x_sqd = sem("x_sqd")
        x_summed = sem("x_summed")
        x_stdd = sem("x_stdd")
        x_invd = sem("x_invd")
        x_nrm = sem("x_nrm")
        x_turned = sem("x_turned")
        x_done = sem("x_done")
        xs_pe = sem("xs_pe")
        xs_done = sem("xs_done")
        turned = sem("turned")
        turned_sb = sem("turned_sb")
        gram_done = sem("gram_done")
        gram_prod = sem("gram_prod")
        gram_sum = sem("gram_sum")
        row_stdd = sem("row_stdd")
        row_invd = sem("row_invd")
        rows_scaled = sem("rows_scaled")
        rows_high = sem("rows_high")
        rows_low = sem("rows_low")
        u_done = sem("u_done")
        u_high = sem("u_high")
        u_low = sem("u_low")
        y_done = sem("y_done")
        y_squared = sem("y_squared")
        y_summed = sem("y_summed")
        y_stdd = sem("y_stdd")
        y_invd = sem("y_invd")
        x_put = sem("x_put")
        items_done = sem("items_done")
        z_done = sem("z_done")
        pairs_done = sem("pairs_done")
        spilled = sem("spilled")
        repacked = sem("repacked")
        packed_high = sem("packed_high")
        packed_low = sem("packed_low")
        sum_put = sem("sum_put")
        o_done = sem("o_done")
        o_squared = sem("o_squared")
        ov_done = sem("ov_done")
        o_stdd = sem("o_stdd")
        o_invd = sem("o_invd")
        zn_done = sem("zn_done")
        h1_done = sem("h1_done")
        h1_relu = sem("h1_relu")
        h2_done = sem("h2_done")
        h2_relu = sem("h2_relu")
        yo_done = sem("yo_done")
        yo_copied = sem("yo_copied")
        stored = sem("stored")

        def wait(eng, s, value):
            if not isinstance(value, int) or value > 0:
                eng.wait_ge(s, value)

        block = ctx.enter_context(nc.Block())

        def passes(eng, body):
            body(0, 0)
            body(1, 1)
            with eng.Fori(1, PASSES // 2 - 1) as n:
                body(2 * n, 0)
                body(2 * n + 1, 1)
            body(PASSES - 2, 0)
            body(PASSES - 1, 1)

        def at_end(i):
            return isinstance(i, int) and i == PASSES - 1

        def at_start(i):
            return isinstance(i, int) and i == 0


        x_slots = {0: 1, 3: 2, 8: 3}
        halves = [slice(0, STEPS // 2), slice(STEPS // 2, STEPS)]

        def prepares(i):
            return isinstance(i, int) and i < 2

        def place(c):
            return 2 * (c % 2) + c // 2

        def head_slots(i, per_slot, s):
            for back, step in per_slot.get(s, ()):
                j = i - back
                if not isinstance(j, int) or 0 <= j < PASSES:
                    step(j)


        @block.sync
        def _(sp):
            def load(s, dst, src):
                sp.dma_start(dst, src).then_inc(s, 16)

            load(w_in[0], ids_raw[:], ids)
            load(w_in[0], size_sb[:], size_c)
            load(w_in[0], base_sb[:], base_c)
            load(w_in[1], ws2[:], wst2)
            load(w_in[1], eye_sb[:], eye)
            load(w_in[1], wsi_sb[:], wsi13)
            load(w_in[1], mask_sb[:], mask13)
            load(w_in[2], wd_sb[:], wdt)
            load(dense_in[0], x_dense, dense[:, :, 0:X_CHUNK])
            load(w_in[2], gs_sb[:], gs_b)
            load(w_in[2], bs_sb[:], bs_b)
            load(w_in[2], pick_sb[:], bs_pick)
            load(w_in[2], gd_sb[:], gd_c)
            load(w_in[2], bd_sb[:], bd_c)
            load(w_in[3], wl_sb[:], wl)
            load(w_in[3], ga_sb[:], ga)
            load(w_in[3], gb_sb[:], gb)
            load(w_in[3], bc_sb[:], bsi_c)
            load(w_in[3], bp_sb[:], bsi_p)
            load(w_in[3], bq_sb[:], bsi_q)
            load(w_in[3], selp_sb, sel_p)
            load(w_in[3], selq_sb, sel_q)
            load(w_in[4], w1_sb[:], w1)
            load(w_in[4], gl_sb[:], gl_c)
            load(w_in[4], bl_sb[:], bl_c)
            load(w_in[4], b1_sb[:], b1_c)
            load(w_in[5], w2_sb[:], w2)
            load(w_in[5], b2_sb[:], b2_c)
            load(w_in[5], w3_sb[:], w3)
            for c in range(1, X_CHUNKS):
                sp.wait_ge(x_pe, c)
                load(dense_in[c], x_dense, dense[:, :, c * X_CHUNK:(c + 1) * X_CHUNK])

            def repack(i, par):
                if at_start(i):
                    sp.wait_ge(x_pe, X_CHUNKS)
                sp.wait_ge(pairs_done, 8 * i + 8)
                load(head_in[par], dense_sb[par], dense[:, :, bass.ds(i * BODY, BODY)])
                wait(sp, packed_low, 3 * i)
                for j in range(4):
                    sp.dma_start(spill[par, :, :, 64 * j:64 * j + 64].rearrange("q p n -> p q n"),
                                 pairs[par][32 * j:32 * j + 32]).then_inc(spilled, 16)
                sp.wait_ge(spilled, 64 * i + 64)
                for p0, q0, nq, step0, row0 in STRIPS:
                    sp.dma_start(packed[row0:row0 + PROJ - p0, step0:step0 + nq, :],
                                 spill[par, 1 + q0:1 + q0 + nq, p0:PROJ].rearrange("q p n -> p q n")
                                 ).then_inc(repacked, 16)
                for row0, q in ((0, 0), (PROJ, ITEMS - 1)):
                    sp.dma_start(packed[row0:row0 + PROJ, LAST, :], spill[par, q]).then_inc(repacked, 16)

            sp.wait_ge(zeroed, 8)
            passes(sp, repack)
            sp.wait_ge(yo_copied, PASSES)
            sp.dma_start(out, y_out[:]).then_inc(stored, 16)
            sp.wait_ge(stored, 16)

        @block.gpsimd
        def _(pool):
            def gather(i, h):
                wait(pool, rows_scaled, 8 * i + 4 * h - 4)
                pool.tensor_copy(idx[h][:], idx_all[:, bass.ds((2 * i + h) * TILES, TILES)]).then_inc(idx_copied, 1)
                pool.wait_ge(idx_copied, 2 * i + h + 1)
                pool.nop(nofuse=True)
                for v, (lo, hi) in enumerate(GROUPS):
                    for t in range(lo, hi):
                        pool.indirect_dma_start(
                            rows[h][:, t, :], None, table,
                            bass.IndirectOffsetOnAxis(ap=idx[h][:, t:t + 1], axis=0)).then_inc(gathered[h][v], 16)

            pool.wait_ge(ids_ready, 7)
            gather(0, 0)
            gather(0, 1)
            with pool.Fori(1, PASSES) as i:
                gather(i, 0)
                gather(i, 1)

        @block.tensor
        def _(pe):
            def transposes(q, k_par, v):
                lo, hi = GROUPS[v]
                n = (hi - lo) // 2
                wait(pe, gram_prod, q)
                for m in range(n):
                    src = rows[k_par][:, lo + 2 * m:lo + 2 * m + 2, :].rearrange("p a d -> p (a d)")
                    ins = nc.tensor.transpose(front_ps[:, m * P:(m + 1) * P], src, eye_sb[:])
                ins.then_inc(turned, 1)

            def gram_mm(q, v):
                lo, hi = GROUPS[v]
                pe.wait_ge(turned_sb, q + 1)
                for m in range((hi - lo) // 2):
                    ins = nc.tensor.matmul(front_ps[:, m * P:(m + 1) * P], rows_t[:, m * P:(m + 1) * P], gram[:],
                                           start=True, stop=True)
                ins.then_inc(gram_done, 1)

            def u_mm(u, v):
                pe.wait_ge(rows_low, u + 1)
                wait(pe, u_low, u)
                ch, w = v // 2, v % 2
                for x in range(UNIT // BANK_B):
                    b0 = w * UNIT + x * BANK_B
                    fresh = True
                    for t in range(CHUNK_TILES):
                        lo, hi = max(tile_first(t), b0), min(tile_last(t) + 1, b0 + BANK_B)
                        if lo >= hi:
                            continue
                        both = rows_s[:, ch * CHUNK_TILES + t, :, :].rearrange("p a d -> p (a d)")
                        for part in (pat_h, pat_l):
                            ins = nc.tensor.matmul(
                                u_ps[:, x, (lo - b0) * PROJ:(hi - b0) * PROJ], both,
                                part[:, t, lo - tile_first(t):hi - tile_first(t), :].rearrange("p s q -> p (s q)"),
                                start=fresh, stop=True, skip_group_check=True)
                            fresh = False
                ins.then_inc(u_done, 1)

            def y_mm(u, par):
                pe.wait_ge(u_low, u + 1)
                wait(pe, items_done, u)
                for x in range(UNIT // BANK_B):
                    cut = slice(x * BANK_B, (x + 1) * BANK_B)
                    high = u_h[par][:, cut, :].rearrange("p b q -> p (b q)")
                    low = u_l[par][:, cut, :].rearrange("p b q -> p (b q)")
                    nc.tensor.matmul(y_ps[:, x, :], ws_h[:], high, start=True, stop=False)
                    nc.tensor.matmul(y_ps[:, x, :], ws_l[:], high, start=False, stop=False)
                    ins = nc.tensor.matmul(y_ps[:, x, :], ws_b[:], low, start=False, stop=True)
                ins.then_inc(y_done, 1)

            def z_mm(u, par):
                pe.wait_ge(items_done, u + 1)
                pe.wait_ge(x_put, u + 1)
                wait(pe, pairs_done, u)
                for g in range(GSLOTS):
                    for j in range(4):
                        t = items[par][:, j * GSLOTS + g, :]
                        ins = nc.tensor.matmul(z_ps[32 * j:32 * j + 32, g * ITEMS:(g + 1) * ITEMS],
                                               t[:, 1:1 + PROJ], t, start=True, stop=True)
                ins.then_inc(z_done, 1)

            def o_mm(i, piece):
                if piece == 0:
                    pe.wait_ge(packed_low, 3 * i + 3)
                    wait(pe, yo_copied, i)
                todo = [(c, st) for c in range(O_CH) for st in range(STEPS)]
                size = -(-len(todo) // 5)
                for c, st in todo[piece * size:(piece + 1) * size]:
                    if c >= 2 and st == 0:
                        pe.wait_ge(o_squared, O_CH * i + c - 1)
                    for m, (w, x) in enumerate(((wl_h, packed_h), (wl_l, packed_h), (wl_h, packed_l))):
                        ins = nc.tensor.matmul(head_ps[:, place(c), :], w[:, st, c * P:(c + 1) * P], x[:, st, :],
                                               start=(st == 0 and m == 0), stop=(st == LAST and m == 2))
                    if st == LAST:
                        ins.then_inc(o_done, 1)

            def ov_mm(i):
                pe.wait_ge(o_squared, O_CH * (i + 1))
                for c in range(O_CH):
                    ins = nc.tensor.matmul(head_ps[:, place(Z_CH), :], ones_sb[:], o_sq[:, c, :],
                                           start=(c == 0), stop=(c == O_CH - 1))
                ins.then_inc(ov_done, 1)

            def h1_mm(i, par, c, parts):
                if c < 2 and parts[0] == 0:
                    pe.wait_ge(o_stdd, i + 1)
                    pe.wait_ge(head_in[par], (i - par + 2) * 8)
                elif parts[0] == 0:
                    pe.wait_ge(h1_relu, 4 * i + c - 1)
                else:
                    pe.wait_ge(zn_done, i + 1)
                for n in parts:
                    m = (n + Z_CH) % (Z_CH + D_CH)
                    x = z_sb[:, m, :] if m < Z_CH else dense_sb[par][:, m - Z_CH, :]
                    ins = nc.tensor.matmul(head_ps[:, place(c), :], w1_sb[:, m, c * P:(c + 1) * P], x,
                                           start=(n == 0), stop=(n == Z_CH + D_CH - 1))
                if parts[-1] == Z_CH + D_CH - 1:
                    ins.then_inc(h1_done, 1)

            def h2_mm(i, c):
                if c == 0:
                    pe.wait_ge(h1_relu, 4 * (i + 1))
                for m in range(4):
                    ins = nc.tensor.matmul(head_ps[:, place(c), :], w2_sb[:, m, c * P:(c + 1) * P], h1_sb[:, m, :],
                                           start=(m == 0), stop=(m == 3))
                ins.then_inc(h2_done, 1)

            def yo_mm(i):
                pe.wait_ge(h2_relu, i + 1)
                for m in range(H2_CH):
                    ins = nc.tensor.matmul(head_ps[0:1, 2, :], w3_sb[:, m:m + 1], h2_sb[:, m, :],
                                           start=(m == 0), stop=(m == H2_CH - 1))
                ins.then_inc(yo_done, 1)

            x_proj = head_ps[:, 0:2, :].rearrange("p a n -> p (a n)")
            x_back = head_ps[:, 2:4, :].rearrange("p a n -> p (a n)")

            def x_mm(c):
                pe.wait_ge(dense_in[c], 16)
                wait(pe, xs_done, c)
                if c == X_CHUNKS - 1:
                    pe.wait_ge(wl_prep, 10)
                for b in range(X_CHUNK // P):
                    for m in range(D_CH):
                        ins = nc.tensor.matmul(x_proj[:, b * P:(b + 1) * P], x_dense[:, m, b * P:(b + 1) * P],
                                               wd_sb[:, m, :], start=(m == 0), stop=(m == D_CH - 1))
                ins.then_inc(x_pe, 1)

            def x_turn(c):
                pe.wait_ge(x_nrm, c + 1)
                for b in range(X_CHUNK // P):
                    ins = nc.tensor.transpose(x_back[:, b * P:(b + 1) * P], x_rows[:, b * P:(b + 1) * P], eye_sb[:])
                ins.then_inc(x_turned, 1)

            def x_sum_mm(c):
                pe.wait_ge(x_done, c + 1)
                nc.tensor.matmul(x_proj[64:65, :], ones_sb[:, 0:1], x_t[:, c * X_CHUNK:(c + 1) * X_CHUNK],
                                 start=True, stop=True).then_inc(xs_pe, 1)

            def head_early(par):
                return {0: [(2, lambda j: o_mm(j, 4))],
                        1: [(2, lambda j: h1_mm(j, par, 0, (0, 1)))],
                        2: [(2, lambda j: h1_mm(j, par, 0, (2, 3, 4)))],
                        3: [(2, lambda j: h1_mm(j, par, 2, (0, 1, 2, 3, 4)))],
                        4: [(2, lambda j: h1_mm(j, par, 3, (2, 3, 4)))], 5: [(2, lambda j: h2_mm(j, 1))],
                        6: [(1, lambda j: o_mm(j, 0))], 7: [(1, lambda j: o_mm(j, 2))]}

            def head_late(par):
                return {0: [(2, ov_mm)], 1: [(2, lambda j: h1_mm(j, par, 1, (0, 1)))],
                        2: [(2, lambda j: h1_mm(j, par, 1, (2, 3, 4)))],
                        3: [(2, lambda j: h1_mm(j, par, 3, (0, 1)))],
                        4: [(2, lambda j: h2_mm(j, 0))], 5: [(2, yo_mm)],
                        6: [(1, lambda j: o_mm(j, 1))], 7: [(1, lambda j: o_mm(j, 3))]}

            def prepare_slot(t):
                wide = [head_ps[32:64, 0:2, :], head_ps[64:65, 2:4, :], head_ps[96:97, 0:2, :]]
                coef, x_coef, const = [t.rearrange("p a n -> p (a n)") for t in wide]
                if t in x_slots:
                    x_mm(x_slots[t])
                elif t - 1 in x_slots:
                    x_turn(x_slots[t - 1])
                elif t - 2 in x_slots:
                    x_sum_mm(x_slots[t - 2])
                if t == 6:
                    pe.wait_ge(wl_prep, 5)
                    pe.wait_ge(xs_done, 3)
                    for st in range(STEPS):
                        ins = nc.tensor.matmul(coef, sel_b[:, st, :], wl_sb[:, st, :],
                                               start=(st == 0), stop=(st == LAST))
                    ins.then_inc(wl_pe, 1)
                    nc.tensor.matmul(x_coef, bc_sb[0:32, :], wl_sb[0:32, LAST, :],
                                     start=True, stop=True).then_inc(wl_pe, 1)
                elif t == 7:
                    pe.wait_ge(wl_prep, 6)
                    nc.tensor.matmul(const, bc_sb[32:64, :], cs_sb[32:64, 0:MAXD],
                                     start=True, stop=True).then_inc(wl_pe, 1)
                elif t == 11:
                    pe.wait_ge(w_in[4], 4 * 16)
                    pe.wait_ge(xs_done, X_CHUNKS)
                    for c in range(4):
                        for m in range(Z_CH):
                            ins = nc.tensor.matmul(head_ps[:, 0, c:c + 1], w1_sb[:, m, c * P:(c + 1) * P],
                                                   bl_sb[:, m:m + 1], start=(m == 0), stop=(m == Z_CH - 1))
                    ins.then_inc(wl_pe, 1)

            def body(i, par):
                for s in range(SLOTS):
                    u = 8 * i + s
                    ahead = not (at_end(i) and s >= 5)
                    y_mm(u, s % 2)
                    if not (at_end(i) and s == SLOTS - 1):
                        u_mm(u + 1, (s + 1) % 4)
                    if ahead:
                        v, h = (s + 3) % 4, (s + 3) // 4
                        pe.wait_ge(gathered[h % 2][v], (i + 1 + h // 2) * 16 * (GROUPS[v][1] - GROUPS[v][0]))
                        transposes(u + 3, h % 2, v)
                    head_slots(i, head_early(par), s)
                    if prepares(i):
                        prepare_slot(u)
                    if ahead:
                        gram_mm(u + 3, v)
                    head_slots(i, head_late(par), s)
                    z_mm(u, s % 2)

            pe.wait_ge(w_in[1], 4 * 16)
            pe.wait_ge(zeroed, 8)
            pe.wait_ge(prep, 2)
            nc.tensor.transpose(y_ps[:, 0, 0:P], ws2[:], eye_sb[:]).then_inc(prep_pe, 1)
            pe.wait_ge(prep, 3)
            nc.tensor.matmul(y_ps[:, 1, 0:P], ws_e[:], ws_e[:], start=True, stop=True).then_inc(prep_pe, 1)
            pe.wait_ge(prep, 7)
            nc.tensor.matmul(u_ps[64:128, 0, 0:PROJ], ones_sb[0:N_SPARSE, 0:64],
                             wsi_sb[0:N_SPARSE, 0, :], start=True, stop=True).then_inc(prep_pe, 1)

            pe.wait_ge(prep, 8)
            x_mm(0)
            x_turn(0)
            x_sum_mm(0)

            for v in range(3):
                pe.wait_ge(gathered[0][v], 16 * (GROUPS[v][1] - GROUPS[v][0]))
                transposes(v, 0, v)
                gram_mm(v, v)
            pe.wait_ge(prep_act, 4)
            pe.wait_ge(prep, 19)
            u_mm(0, 0)

            passes(pe, body)
            for i, par in ((PASSES, 0), (PASSES + 1, 1)):
                for s in range(SLOTS):
                    head_slots(i, head_early(par), s)
                    head_slots(i, head_late(par), s)

        @block.scalar
        def _(act):
            def turn_copy(q, v):
                n = (GROUPS[v][1] - GROUPS[v][0]) // 2 * P
                act.wait_ge(turned, q + 1)
                wait(act, gram_done, q)
                nc.scalar.activation(rows_t[:, 0:n], front_ps[:, 0:n], ACT.Copy).then_inc(turned_sb, 1)

            def row_std_f(q, v):
                n = GROUPS[v][1] - GROUPS[v][0]
                act.wait_ge(gram_sum, q + 1)
                wait(act, row_invd, q)
                nc.scalar.activation(row_std[:, 0:n], row_var[:, 0:n], ACT.Sqrt, bias=eps_sb[:],
                                     scale=1.0 / E_DIM).then_inc(row_stdd, 1)

            def rows_high_f(q, v):
                lo, hi = GROUPS[v]
                act.wait_ge(rows_scaled, q + 1)
                wait(act, u_done, q - (2 if v < 3 else 3))
                nc.scalar.activation(rows_s[:, lo:hi, 0, :], rows_f[:, 0:hi - lo, :],
                                     ACT.Copy).then_inc(rows_high, 1)

            def u_high_f(u, par):
                act.wait_ge(u_done, u + 1)
                wait(act, y_done, u - 1)
                nc.scalar.activation(u_h[par][:].rearrange("p b q -> p (b q)"),
                                     u_ps[:].rearrange("p a n -> p (a n)"), ACT.Copy).then_inc(u_high, 1)

            def put_x(u, par, i, h, v):
                wait(act, z_done, u - 1)
                src = x_t[:, bass.ds(i * BODY, BODY)].rearrange("p (j h v g) -> p h v j g", j=4, h=2, v=4)[:, h, v]
                nc.scalar.activation(items[par][:, :, 0].rearrange("p (j g) -> p j g", j=4), src,
                                     ACT.Copy).then_inc(x_put, 1)

            def y_square(u):
                act.wait_ge(y_done, u + 1)
                wait(act, y_summed, u)
                nc.scalar.activation(y_sq[:].rearrange("p b q -> p (b q)"),
                                     y_ps[:].rearrange("p a n -> p (a n)"), ACT.Square).then_inc(y_squared, 1)

            def y_std_f(u):
                act.wait_ge(y_summed, u + 1)
                wait(act, y_invd, u)
                nc.scalar.activation(y_std[:], y_sum[:], ACT.Sqrt, bias=eps_sb[:],
                                     scale=1.0 / PROJ).then_inc(y_stdd, 1)

            def z_copy(u, par, s):
                act.wait_ge(z_done, u + 1)
                nc.scalar.activation(
                    pairs[par][:, :, s * GSLOTS:(s + 1) * GSLOTS].rearrange("p q g -> p g q"),
                    z_ps[:, 0:GSLOTS * ITEMS].rearrange("p (g q) -> p g q", q=ITEMS),
                    ACT.Copy).then_inc(pairs_done, 1)

            def sum_put_f(i):
                nc.scalar.activation(packed[ROW_SUM:ROW_SUM + 1, LAST, :],
                                     x_sum[:, bass.ds(i * BODY, BODY)], ACT.Copy).then_inc(sum_put, 1)

            def packed_high_f(i, part):
                if part == 0:
                    act.wait_ge(repacked, (i + 1) * PACK_DMAS * 16)
                    act.wait_ge(sum_put, i + 1)
                steps = slice(STEPS * part // 3, STEPS * (part + 1) // 3)
                nc.scalar.activation(packed_h[:, steps, :], packed[:, steps, :], ACT.Copy).then_inc(packed_high, 1)

            def o_square(i, c):
                act.wait_ge(o_done, O_CH * i + c + 1)
                ins = nc.scalar.activation(o_sq[:, c, :], head_ps[:, place(c), :], ACT.Square)
                if c < Z_CH:
                    ins = nc.scalar.activation(o_sb[:, c, :], head_ps[:, place(c), :], ACT.Copy)
                ins.then_inc(o_squared, 1)

            def o_std_f(i):
                act.wait_ge(ov_done, i + 1)
                nc.scalar.activation(o_std, head_ps[:, place(Z_CH), :], ACT.Sqrt, bias=eps_sb[:],
                                     scale=1.0 / MAXD).then_inc(o_stdd, 1)

            def h1_act(i, c):
                act.wait_ge(h1_done, 4 * i + c + 1)
                nc.scalar.activation(h1_sb[:, c, :], head_ps[:, place(c), :], ACT.Relu, bias=b1f[:, c:c + 1]).then_inc(h1_relu, 1)

            def h2_act(i):
                act.wait_ge(h2_done, H2_CH * (i + 1))
                for c in range(H2_CH):
                    ins = nc.scalar.activation(h2_sb[:, c, :], head_ps[:, place(c), :], ACT.Relu, bias=b2_sb[:, c:c + 1])
                ins.then_inc(h2_relu, 1)

            def yo_copy(i):
                act.wait_ge(yo_done, i + 1)
                nc.scalar.activation(y_out[:, bass.ds(i * BODY, BODY)], head_ps[0:1, 2, :],
                                     ACT.Copy).then_inc(yo_copied, 1)

            head_early = {0: [(2, lambda j: o_square(j, 2))], 1: [(2, o_std_f), (1, sum_put_f)],
                          3: [(2, lambda j: h1_act(j, 1))], 4: [(1, lambda j: packed_high_f(j, 0))],
                          5: [(1, lambda j: packed_high_f(j, 2))], 6: [(2, yo_copy)], 7: [(1, lambda j: o_square(j, 0))]}
            head_late = {0: [(2, lambda j: o_square(j, 3))], 2: [(2, lambda j: h1_act(j, 0))],
                         3: [(2, lambda j: h1_act(j, 2))],
                         4: [(2, lambda j: h1_act(j, 3)), (1, lambda j: packed_high_f(j, 1))], 5: [(2, h2_act)],
                         7: [(1, lambda j: o_square(j, 1))]}

            def prepare_slot(t):
                if t in x_slots:
                    x_square(x_slots[t])
                elif t - 1 in x_slots:
                    x_copy(x_slots[t - 1])
                elif t - 2 in x_slots:
                    x_sum_copy(x_slots[t - 2])
                if t in (8, 9):
                    act.wait_ge(wl_prep, 10)
                    nc.scalar.activation(wl_h[:, halves[t - 8], :], wl_sb[:, halves[t - 8], :],
                                         ACT.Copy).then_inc(wl_act, 1)

            def body(i, par):
                for s in range(SLOTS):
                    u = 8 * i + s
                    split = not (at_end(i) and s >= 6)
                    head_slots(i, head_early, s)
                    if prepares(i) and u - 1 in x_slots:
                        x_std_f(x_slots[u - 1])
                    if not (at_start(i) and s == 0):
                        z_copy(u - 1, par if s else 1 - par, (s - 1) % 8)
                    put_x(u, s % 2, i, s // 4, s % 4)
                    if split:
                        row_std_f(u + 2, (s + 2) % 4)
                    y_square(u)
                    if split:
                        rows_high_f(u + 2, (s + 2) % 4)
                    if not (at_end(i) and s == SLOTS - 1):
                        u_high_f(u + 1, 1 - s % 2)
                    y_std_f(u)
                    if not (at_end(i) and s >= 5):
                        turn_copy(u + 3, (s + 3) % 4)
                    head_slots(i, head_late, s)
                    if prepares(i):
                        prepare_slot(u)

            x_proj = head_ps[:, 0:2, :].rearrange("p a n -> p (a n)")
            x_back = head_ps[:, 2:4, :].rearrange("p a n -> p (a n)")

            def x_square(c):
                act.wait_ge(x_pe, c + 1)
                wait(act, x_summed, c)
                nc.scalar.activation(x_sq, x_proj, ACT.Square).then_inc(x_sqd, 1)

            def x_std_f(c):
                act.wait_ge(x_summed, c + 1)
                wait(act, x_invd, c)
                nc.scalar.activation(x_std[:], x_var[:], ACT.Sqrt, bias=eps_sb[:],
                                     scale=1.0 / E_DIM).then_inc(x_stdd, 1)

            def x_copy(c):
                act.wait_ge(x_turned, c + 1)
                nc.scalar.activation(x_t[:, c * X_CHUNK:(c + 1) * X_CHUNK], x_back, ACT.Identity, bias=bd_sb[:],
                                     scale=gd_sb[:]).then_inc(x_done, 1)

            def x_sum_copy(c):
                act.wait_ge(xs_pe, c + 1)
                nc.scalar.activation(x_sum[:, c * X_CHUNK:(c + 1) * X_CHUNK], x_proj[64:65, :],
                                     ACT.Copy).then_inc(xs_done, 1)

            act.wait_ge(zeroed, 8)
            act.wait_ge(w_in[2], 6 * 16)
            nc.scalar.activation(bs_h[:], bs_sb[:], ACT.Copy).then_inc(prep_act, 1)
            act.wait_ge(prep, 6)
            nc.scalar.activation(ws_h[:], ws_g[:], ACT.Copy).then_inc(prep_act, 1)
            act.wait_ge(prep_pe, 3)
            nc.scalar.activation(wss_h[64:128, :], u_ps[64:128, 0, 0:PROJ], ACT.Copy).then_inc(prep_act, 1)
            act.wait_ge(prep, 9)
            nc.scalar.activation(pat_h[:], pat[:], ACT.Copy).then_inc(prep_act, 1)
            x_square(0)
            x_std_f(0)
            x_copy(0)
            x_sum_copy(0)
            for v in range(3):
                turn_copy(v, v)
                if v < 2:
                    row_std_f(v, v)
                    rows_high_f(v, v)
            act.wait_ge(prep, 19)
            u_high_f(0, 0)
            act.wait_ge(w_in[5], 3 * 16)
            passes(act, body)
            z_copy(UNITS * BLOCKS - 1, 1, 7)
            for i in (PASSES, PASSES + 1):
                for s in range(SLOTS):
                    head_slots(i, head_early, s)
                    head_slots(i, head_late, s)

        @block.vector
        def _(dve):
            V = nc.vector

            def gram_reduce(q, k_par, v):
                lo, hi = GROUPS[v]
                n = hi - lo
                pr = prod[:, 0:n * D_SPARSE].rearrange("p (t d) -> p t d", d=D_SPARSE)
                dve.wait_ge(gram_done, q + 1)
                V.tensor_tensor(pr, front_ps[:, 0:n * D_SPARSE].rearrange("p (t d) -> p t d", d=D_SPARSE),
                                rows[k_par][:, lo:hi, :], ALU.mult).then_inc(gram_prod, 1)
                dve.wait_ge(gram_prod, q + 1)
                V.tensor_reduce(out=row_var[:, 0:n], in_=pr, axis=AX, op=ALU.add).then_inc(gram_sum, 1)

            def scale_rows(q, k_par, v):
                lo, hi = GROUPS[v]
                n = hi - lo
                dve.wait_ge(row_stdd, q + 1)
                V.reciprocal(row_inv[:, 0:n], row_std[:, 0:n]).then_inc(row_invd, 1)
                dve.wait_ge(row_invd, q + 1)
                wait(dve, rows_low, q)
                V.tensor_tensor(rows_f[:, 0:n, :], rows[k_par][:, lo:hi, :],
                                row_inv[:, 0:n].unsqueeze(2).to_broadcast([P, n, D_SPARSE]),
                                ALU.mult).then_inc(rows_scaled, 1)

            def rows_low_f(q, v):
                lo, hi = GROUPS[v]
                dve.wait_ge(rows_high, q + 1)
                V.tensor_tensor(rows_s[:, lo:hi, 1, :], rows_f[:, 0:hi - lo, :],
                                rows_s[:, lo:hi, 0, :].bitcast(fp32), ALU.subtract).then_inc(rows_low, 1)

            def u_low_f(u, par):
                dve.wait_ge(u_high, u + 1)
                wait(dve, y_done, u - 1)
                V.tensor_tensor(u_l[par][0:64].rearrange("p b q -> p (b q)"),
                                u_ps[0:64].rearrange("p a n -> p (a n)"),
                                u_h[par][0:64].rearrange("p b q -> p (b q)").bitcast(fp32),
                                ALU.subtract).then_inc(u_low, 1)

            def y_reduce(u):
                dve.wait_ge(y_squared, u + 1)
                wait(dve, y_stdd, u)
                V.tensor_reduce(out=y_sum[:], in_=y_sq[:], axis=AX, op=ALU.add).then_inc(y_summed, 1)

            def normalise(u, par):
                dve.wait_ge(y_stdd, u + 1)
                V.reciprocal(y_inv[:], y_std[:]).then_inc(y_invd, 1)
                dve.wait_ge(y_invd, u + 1)
                wait(dve, z_done, u - 1)
                V.tensor_tensor(items[par][:, :, 1:1 + PROJ], y_ps[:].rearrange("p a (b q) -> p (a b) q", q=PROJ),
                                y_inv[:].unsqueeze(2).to_broadcast([P, UNIT, PROJ]), ALU.mult).then_inc(items_done, 1)

            def packed_low_f(i, part):
                dve.wait_ge(packed_high, 3 * i + part + 1)
                steps = slice(STEPS * part // 3, STEPS * (part + 1) // 3)
                V.tensor_tensor(packed_l[:, steps, :], packed[:, steps, :], packed_h[:, steps, :].bitcast(fp32),
                                ALU.subtract).then_inc(packed_low, 1)

            def o_inv_f(i, half):
                dve.wait_ge(o_stdd, i + 1)
                cut = slice(half * BODY // 2, (half + 1) * BODY // 2)
                V.reciprocal(o_inv[:, cut], o_std[:, cut]).then_inc(o_invd, 1)

            def z_norm(i):
                dve.wait_ge(o_invd, 2 * (i + 1))
                V.tensor_tensor(z_sb[:], o_sb[:], o_inv.unsqueeze(1).to_broadcast([P, Z_CH, BODY]),
                                ALU.mult).then_inc(zn_done, 1)

            x_proj = head_ps[:, 0:2, :].rearrange("p a n -> p (a n)")

            def x_reduce(c):
                dve.wait_ge(x_sqd, c + 1)
                wait(dve, x_stdd, c)
                V.tensor_reduce(out=x_var[:], in_=x_sq.rearrange("p (b e) -> p b e", e=E_DIM), axis=AX,
                                op=ALU.add).then_inc(x_summed, 1)
                dve.wait_ge(x_summed, c + 1)

            def x_norm(c):
                dve.wait_ge(x_stdd, c + 1)
                V.reciprocal(x_inv[:], x_std[:]).then_inc(x_invd, 1)
                dve.wait_ge(x_invd, c + 1)
                wait(dve, x_turned, c)
                V.tensor_tensor(x_rows.rearrange("p (b e) -> p b e", e=E_DIM),
                                x_proj.rearrange("p (b e) -> p b e", e=E_DIM),
                                x_inv[:].unsqueeze(2).to_broadcast([P, X_CHUNK // P, E_DIM]),
                                ALU.mult).then_inc(x_nrm, 1)

            head_early = {1: [(2, lambda j: o_inv_f(j, 0))], 2: [(2, z_norm)], 5: [(1, lambda j: packed_low_f(j, 1))]}
            head_late = {1: [(2, lambda j: o_inv_f(j, 1))], 4: [(1, lambda j: packed_low_f(j, 0))],
                         5: [(1, lambda j: packed_low_f(j, 2))]}

            def prepare_slot(t):
                wide = [head_ps[32:64, 0:2, :], head_ps[64:65, 2:4, :], head_ps[96:97, 0:2, :]]
                coef, x_coef, const = [t.rearrange("p a n -> p (a n)") for t in wide]
                if t in x_slots:
                    x_reduce(x_slots[t])
                if t in (0, 1):
                    dve.wait_ge(w_in[3], 8 * 16)
                    V.tensor_reduce(out=wl_mean[:, halves[t]], in_=wl_sb[:, halves[t], :], axis=AX,
                                    op=ALU.add).then_inc(wl_sum, 1)
                    if t == 1:
                        dve.wait_ge(wl_sum, 2)
                        V.tensor_scalar(wl_mean[:], wl_mean[:], 1.0 / MAXD, None, ALU.mult).then_inc(wl_sum, 1)
                        V.tensor_tensor(fac[:], ga_sb[:], gb_sb[:], ALU.mult).then_inc(wl_sum, 1)
                elif t in (2, 3):
                    dve.wait_ge(wl_sum, 4)
                    half = wl_sb[:, halves[t - 2], :]
                    V.tensor_tensor(half, half, wl_mean[:, halves[t - 2]].unsqueeze(2).to_broadcast(
                        [P, half.shape[1], MAXD]), ALU.subtract).then_inc(wl_prep, 1)
                elif t == 4:
                    sel = [P, STEPS, PROJ]
                    V.tensor_tensor(sel_a, selp_sb, bq_sb[:].unsqueeze(2).to_broadcast(sel),
                                    ALU.mult).then_inc(wl_prep, 1)
                    V.tensor_tensor(sel_b, selq_sb, bp_sb[:].unsqueeze(2).to_broadcast(sel),
                                    ALU.mult).then_inc(wl_prep, 1)
                    dve.wait_ge(wl_prep, 4)
                    V.tensor_tensor(sel_b, sel_b, sel_a, ALU.add).then_inc(wl_prep, 1)
                elif t == 6:
                    dve.wait_ge(wl_pe, 2)
                    V.tensor_copy(cs_sb[32:64, 0:MAXD], coef).then_inc(wl_prep, 1)
                if t in (6, 7):
                    half = wl_sb[:, halves[t - 6], :]
                    V.tensor_tensor(half, half, fac[:, halves[t - 6]].unsqueeze(2).to_broadcast(
                        [P, half.shape[1], MAXD]), ALU.mult).then_inc(wl_prep, 1)
                if t == 7:
                    dve.wait_ge(wl_pe, 3)
                    dve.wait_ge(wl_prep, 8)
                    V.tensor_scalar(wl_sb[32:64, LAST, :], cs_sb[32:64, 0:MAXD], ga_sb[32:64, LAST:STEPS], None, ALU.mult)
                    V.tensor_copy(wl_sb[ROW_SUM:ROW_SUM + 1, LAST, :], x_coef).then_inc(wl_prep, 1)
                    V.tensor_scalar(wl_sb[ROW_ONE:ROW_ONE + 1, LAST, :], const, float(E_DIM) / 2.0, None,
                                    ALU.mult).then_inc(wl_prep, 1)
                elif t in (9, 10):
                    half = halves[t - 9]
                    dve.wait_ge(wl_act, t - 8)
                    V.tensor_tensor(wl_l[:, half, :], wl_sb[:, half, :], wl_h[:, half, :].bitcast(fp32),
                                    ALU.subtract).then_inc(wl_prep, 1)
                elif t == 11:
                    dve.wait_ge(wl_pe, 4)
                    V.tensor_tensor(b1f[:], head_ps[:, 0, 0:4], b1_sb[:], ALU.add).then_inc(wl_prep, 1)
                    V.tensor_tensor(w1_sb[:, 0:Z_CH, :], w1_sb[:, 0:Z_CH, :],
                                    gl_sb[:].unsqueeze(2).to_broadcast([P, Z_CH, H1]), ALU.mult).then_inc(wl_prep, 1)

            def body(i, par):
                for s in range(SLOTS):
                    u = 8 * i + s
                    split = not (at_end(i) and s >= 6)
                    h, v = (s + 2) // 4 % 2, (s + 2) % 4
                    if split:
                        gram_reduce(u + 2, h, v)
                        scale_rows(u + 2, h, v)
                    head_slots(i, head_early, s)
                    if prepares(i) and u - 1 in x_slots:
                        x_norm(x_slots[u - 1])
                    y_reduce(u)
                    if split:
                        rows_low_f(u + 2, v)
                    normalise(u, s % 2)
                    if not (at_end(i) and s == SLOTS - 1):
                        u_low_f(u + 1, 1 - s % 2)
                    head_slots(i, head_late, s)
                    if prepares(i):
                        prepare_slot(u)

            V.memset(eps_sb[:], EPS).then_inc(zeroed, 1)
            V.memset(ones_sb[:], 1.0).then_inc(zeroed, 1)
            V.memset(gram[:], 0.0).then_inc(zeroed, 1)
            V.memset(packed[64:128, LAST, :], 0.0).then_inc(zeroed, 1)
            V.memset(packed[96:128, 0:LAST, :], 0.0).then_inc(zeroed, 1)
            V.memset(items[0][:, :, ITEMS - 1], 1.0).then_inc(zeroed, 1)
            V.memset(items[1][:, :, ITEMS - 1], 1.0).then_inc(zeroed, 1)
            dve.wait_ge(zeroed, 7)
            V.memset(packed[ROW_ONE:ROW_ONE + 1, LAST, :], 1.0).then_inc(zeroed, 1)

            dve.wait_ge(w_in[0], 3 * 16)
            three = [P, BLOCKS * 2, CHUNK_TILES]

            def by_tile(t):
                return t.rearrange("p (c t) -> p c t", t=CHUNK_TILES)

            def const(t):
                return t[:].unsqueeze(1).to_broadcast(three)

            V.tensor_scalar(last_sb[:], size_sb[:], -1.0, None, ALU.add).then_inc(ids_ready, 1)
            V.tensor_scalar(ids_f[:], ids_raw[:], 0.0, None, ALU.is_lt).then_inc(ids_ready, 1)
            dve.wait_ge(ids_ready, 2)
            V.tensor_tensor(by_tile(ids_g), by_tile(ids_f), const(size_sb), ALU.mult).then_inc(ids_ready, 1)
            dve.wait_ge(ids_ready, 3)
            V.tensor_tensor(ids_f[:], ids_raw[:], ids_g[:], ALU.add).then_inc(ids_ready, 1)
            dve.wait_ge(ids_ready, 4)
            V.tensor_scalar(ids_g[:], ids_f[:], 0.0, None, ALU.max).then_inc(ids_ready, 1)
            dve.wait_ge(ids_ready, 5)
            V.tensor_tensor(by_tile(ids_f), by_tile(ids_g), const(last_sb), ALU.min).then_inc(ids_ready, 1)
            dve.wait_ge(ids_ready, 6)
            V.tensor_tensor(by_tile(idx_all[:]), by_tile(ids_f), const(base_sb), ALU.add).then_inc(ids_ready, 1)

            dve.wait_ge(w_in[1], 4 * 16)
            V.tensor_reduce(out=ws_mean[:], in_=ws2[:], axis=AX, op=ALU.add).then_inc(sums, 1)
            dve.wait_ge(sums, 1)
            V.tensor_scalar(ws_mean[:], ws_mean[:], 1.0 / E_DIM, None, ALU.mult).then_inc(prep, 1)
            dve.wait_ge(prep, 1)
            V.tensor_scalar(ws2[:], ws2[:], ws_mean[:], None, ALU.subtract).then_inc(prep, 1)
            dve.wait_ge(prep_pe, 1)
            V.tensor_copy(ws_e[:], y_ps[:, 0, 0:P]).then_inc(prep, 1)
            V.tensor_reduce(out=wsi_mean[:], in_=wsi_sb[:], axis=AX, op=ALU.add).then_inc(sums, 1)
            dve.wait_ge(prep_pe, 2)
            V.tensor_copy(gram[0:64, 0:64], y_ps[0:64, 1, 0:64]).then_inc(prep, 1)
            V.tensor_copy(gram[64:128, 64:128], y_ps[64:128, 1, 64:128]).then_inc(prep, 1)
            dve.wait_ge(w_in[2], 6 * 16)
            V.tensor_tensor(ws_g[:], ws2[:], gs_sb[:], ALU.mult).then_inc(prep, 1)

            dve.wait_ge(sums, 2)
            V.tensor_scalar(wsi_mean[:], wsi_mean[:], 1.0 / PROJ, None, ALU.mult).then_inc(sums, 1)
            V.tensor_reduce(out=wd_mean[:], in_=wd_sb[:], axis=AX, op=ALU.add).then_inc(sums, 1)
            dve.wait_ge(sums, 4)
            V.tensor_tensor(wsi_sb[:], wsi_sb[:], wsi_mean[:].unsqueeze(2).to_broadcast(
                [P, CHUNK_TILES, PROJ]), ALU.subtract).then_inc(prep, 1)
            V.tensor_scalar(wd_mean[:], wd_mean[:], 1.0 / E_DIM, None, ALU.mult).then_inc(sums, 1)
            dve.wait_ge(sums, 5)
            V.tensor_tensor(wd_sb[:], wd_sb[:], wd_mean[:].unsqueeze(2).to_broadcast([P, D_CH, E_DIM]),
                            ALU.subtract).then_inc(prep, 1)
            dve.wait_ge(prep, 7)
            four = [P, CHUNK_TILES, SPAN, PROJ]
            V.tensor_tensor(pat[:], wsi_sb[:].unsqueeze(2).to_broadcast(four),
                            mask_sb[:].unsqueeze(3).to_broadcast(four), ALU.mult).then_inc(prep, 1)

            dve.wait_ge(prep_act, 3)
            for h in range(2):
                V.tensor_copy(u_l[h][64:96], wss_h[64:96, :].bitcast(fp32).unsqueeze(1).to_broadcast(
                    [32, UNIT, PROJ])).then_inc(prep, 1)
            V.tensor_tensor(wss_l[64:128, :], u_ps[64:128, 0, 0:PROJ], wss_h[64:128, :].bitcast(fp32),
                            ALU.subtract).then_inc(prep, 1)
            dve.wait_ge(prep, 12)
            for h in range(2):
                V.tensor_copy(u_l[h][96:128], wss_l[96:128, :].unsqueeze(1).to_broadcast(
                    [32, UNIT, PROJ])).then_inc(prep, 1)
            V.tensor_tensor(ws_l[:], ws_g[:], ws_h[:].bitcast(fp32), ALU.subtract).then_inc(prep, 1)
            V.tensor_copy(ws_b[0:64, :], ws_h[0:64, :].bitcast(fp32)).then_inc(prep, 1)
            V.tensor_tensor(bs_t[:], bs_sb[:], bs_h[:].bitcast(fp32), ALU.subtract).then_inc(sums, 1)
            V.tensor_scalar(bs_u[:], bs_h[:].bitcast(fp32), pick_sb[:, 0:1], None, ALU.mult).then_inc(sums, 1)
            dve.wait_ge(sums, 7)
            V.tensor_scalar(bs_t[:], bs_t[:], pick_sb[:, 1:2], None, ALU.mult).then_inc(prep, 1)
            dve.wait_ge(prep, 17)
            V.tensor_tensor(ws_b[64:128, :], bs_t[64:128, :], bs_u[64:128, :], ALU.add).then_inc(prep, 1)
            x_reduce(0)
            dve.wait_ge(prep_act, 4)
            V.tensor_tensor(pat_l[:], pat[:], pat_h[:].bitcast(fp32), ALU.subtract).then_inc(prep, 1)
            x_norm(0)

            for v in range(2):
                gram_reduce(v, 0, v)
                scale_rows(v, 0, v)
                rows_low_f(v, v)
            u_low_f(0, 0)

            passes(dve, body)
            for i in (PASSES, PASSES + 1):
                for s in range(SLOTS):
                    head_slots(i, head_early, s)
                    head_slots(i, head_late, s)




def kernel(**inputs):
    import numpy as np
    import concourse.bacc as bacc
    from concourse import mybir as _mybir
    from concourse.bass_utils import run_bass_kernel_spmd as run

    a = {k: np.asarray(v) for k, v in inputs.items()}
    f32 = np.float32
    tile_rows = np.arange(CHUNK * N_SPARSE).reshape(CHUNK_TILES, P).T
    of_table, of_sample = tile_rows % N_SPARSE, tile_rows // N_SPARSE
    sizes = np.array([a[f"tbl_{n}"].shape[0] for n in range(N_SPARSE)])
    firsts = np.concatenate([[0], np.cumsum(sizes)[:-1]])
    first_of = np.array([tile_first(t) for t in range(CHUNK_TILES)])
    mask = (of_sample - first_of)[:, :, None] == np.arange(SPAN)[None, None, :]

    part = np.arange(P)
    p_of = np.zeros((P, STEPS), int)
    q_of = np.zeros((P, STEPS), int)
    valid = np.zeros((P, STEPS), bool)
    for p0, q0, nq, step0, row0 in STRIPS:
        n = PROJ - p0
        p_of[row0:row0 + n, step0:step0 + nq] = p0 + np.arange(n)[:, None]
        q_of[row0:row0 + n, step0:step0 + nq] = q0 + np.arange(nq)[None, :]
        valid[row0:row0 + n, step0:step0 + nq] = True
    valid &= p_of > q_of
    wl_t = a["L0_rec_Wl"].T
    wl = np.zeros((P, STEPS, MAXD), f32)
    wl[valid] = wl_t[((p_of + 1) * p_of // 2 + q_of + 1)[valid]]
    one = np.arange(PROJ)
    wl[0:PROJ, LAST, :] = wl_t[(one + 1) * one // 2]
    gsi, bsi = a["L0_rec_gsi"], a["L0_rec_bsi"]
    ga = gsi[p_of]
    gb = gsi[q_of]
    ga[0:2 * PROJ, LAST] = gsi[part[0:2 * PROJ] % PROJ]
    gb[0:2 * PROJ, LAST] = 1.0
    place = valid[:, :, None]
    bs_pick = np.zeros((P, 2), f32)
    bs_pick[64, 0] = bs_pick[96, 0] = bs_pick[65, 1] = 1.0
    dense_t = a["r_dense_t"].T.reshape(D_CH, P, PASSES, 2, UNITS, 4, GSLOTS).transpose(1, 0, 2, 5, 3, 4, 6)
    w1 = a["W_top1"].reshape(6, P, H1).transpose(1, 0, 2)[:, [0, 1, 2, 4, 5]]

    given = {
        "table": np.concatenate([a[f"tbl_{n}"] for n in range(N_SPARSE)], axis=0),
        "ids": a["ids"].reshape(BLOCKS * TILES, P).T,
        "dense": dense_t.reshape(P, D_CH, BATCH),
        "size_c": sizes[of_table].astype(f32),
        "base_c": firsts[of_table].astype(f32),
        "eye": np.eye(P, dtype=f32),
        "mask13": mask.astype(f32),
        "sel_p": ((p_of[:, :, None] == one) & place).astype(f32),
        "sel_q": ((q_of[:, :, None] == one) & place).astype(f32),
        "wst2": np.concatenate([a["L0_rec_Ws"].T] * 2, axis=0),
        "gs_b": np.broadcast_to(a["L0_rec_gs"], (P, E_DIM)),
        "bs_b": np.broadcast_to(a["L0_rec_bs"], (P, E_DIM)),
        "bs_pick": bs_pick,
        "wdt": a["L0_rec_Wd"].T.reshape(D_CH, P, E_DIM).transpose(1, 0, 2),
        "gd_c": a["L0_rec_gd"].reshape(P, 1),
        "bd_c": a["L0_rec_bd"].reshape(P, 1),
        "wsi13": a["L0_rec_Wsi"].T[of_table],
        "wl": wl, "ga": ga, "gb": gb,
        "bsi_c": bsi[part % PROJ].reshape(P, 1),
        "bsi_p": bsi[p_of],
        "bsi_q": bsi[q_of],
        "gl_c": a["L0_rec_gl"][0:DIMS_IN_USE].reshape(Z_CH, P).T,
        "bl_c": a["L0_rec_bl"][0:DIMS_IN_USE].reshape(Z_CH, P).T,
        "w1": w1,
        "b1_c": a["b_top1"].reshape(4, P).T,
        "w2": a["W_top2"].reshape(4, P, H2).transpose(1, 0, 2),
        "b2_c": a["b_top2"].reshape(H2_CH, P).T,
        "w3": a["W_top3"].reshape(H2_CH, P).T,
    }
    nc = bacc.Bacc("TRN2", target_bir_lowering=False, num_devices=1)
    arrays, args = {}, {}
    for name, v in given.items():
        v = np.ascontiguousarray(v)
        arrays[f"in_{name}"] = v
        args[name] = nc.dram_tensor(f"in_{name}", v.shape, _mybir.dt.from_np(v.dtype), kind="ExternalInput").ap()
    out = nc.dram_tensor("out_y", (1, BATCH), _mybir.dt.float32, kind="ExternalOutput").ap()
    spill = nc.dram_tensor("spill", (2, ITEMS, PROJ, BODY), _mybir.dt.float32, kind="Internal").ap()
    build_program(nc, spill=spill, out=out, **args)
    r = run(nc, [arrays], core_ids=[0])
    y = r.results[0]["out_y"].reshape(PASSES, 4, 2, UNITS, GSLOTS).transpose(0, 2, 3, 1, 4)
    return y.reshape(BATCH, 1)
```

```python
from contextlib import ExitStack

import concourse.bass as bass
from concourse import mybir

BATCH = 2048
N_SPARSE = 26
D_SPARSE = 64
D_DENSE = 256
E_DIM = 128
PROJ = 32
N_FLAT = 528
MAXD = 512
DIMS_IN_USE = 384
H1, H2 = 512, 256
EPS = 1e-05

P = 128
BLK = 128
BLOCKS = BATCH // BLK
TILES = BLK * N_SPARSE // P
CHUNK = 64
CHUNK_TILES = CHUNK * N_SPARSE // P
UNIT = 32
UNITS = BLK // UNIT
BANK_B = 512 // PROJ
SPAN = -(-(P + N_SPARSE - 1) // N_SPARSE)
GROUPS = [(0, 8), (8, 14), (14, 20), (20, 26)]
ITEMS = PROJ + 2
GSLOTS = UNIT // 4
STEPS = 5
LAST = STEPS - 1
STRIPS = [(1, 0, 4, 0, 0), (5, 4, 4, 0, 31), (9, 8, 4, 0, 58), (13, 12, 4, 0, 81), (17, 16, 4, 0, 100),
          (21, 20, 4, 0, 115)]
STRIPS += [(25, 24 + n, 1, LAST, 65 + 7 * n) for n in range(4)] + [(29, 28 + n, 1, LAST, 97 + 3 * n) for n in range(4)]
ROW_SUM, ROW_ONE = 64, 96
BODY = 2 * BLK
PASSES = BATCH // BODY
SLOTS = BODY // UNIT
O_CH = MAXD // P
Z_CH = DIMS_IN_USE // P
D_CH = D_DENSE // P
X_CHUNK = 512
X_CHUNKS = BATCH // X_CHUNK
H2_CH = H2 // P
PACK_DMAS = len(STRIPS) + 2


def tile_first(t):
    return t * P // N_SPARSE


def tile_last(t):
    return (t * P + P - 1) // N_SPARSE


def build_program(nc, table, ids, dense, size_c, base_c, eye, mask13, sel_p, sel_q,
                  wst2, gs_b, bs_b, wdt, gd_c, bd_c, wsi13, wl, ga, gb, bsi_c, bsi_p, bsi_q, bs_pick,
                  gl_c, bl_c, w1, b1_c, w2, b2_c, w3, spill, out):
    fp32 = mybir.dt.float32
    f32r = mybir.dt.float32r
    i32 = mybir.dt.int32
    ALU = mybir.AluOpType
    ACT = mybir.ActivationFunctionType
    AX = mybir.AxisListType.X

    with ExitStack() as ctx:
        def sb(name, shape, dt=fp32):
            return ctx.enter_context(nc.sbuf_tensor(name, shape, dt))

        def ps(name, shape):
            return ctx.enter_context(nc.psum_tensor(name, shape, fp32))

        def sem(name):
            return ctx.enter_context(nc.semaphore(name))

        ids_raw = sb("ids_raw", [P, BLOCKS * TILES], i32)
        idx_all = sb("idx_all", [P, BLOCKS * TILES], i32)
        size_sb = sb("size_sb", [P, CHUNK_TILES])
        last_sb = sb("last_sb", [P, CHUNK_TILES])
        base_sb = sb("base_sb", [P, CHUNK_TILES])
        idx = [sb(f"idx{h}", [P, TILES], i32) for h in range(2)]
        rows = [sb(f"rows{h}", [P, TILES, D_SPARSE]) for h in range(2)]
        rows_f = sb("rows_f", [P, 8, D_SPARSE])
        rows_s = sb("rows_s", [P, TILES, 2, D_SPARSE], f32r)
        rows_t = sb("rows_t", [P, 4 * P])
        prod = sb("prod", [P, 8 * D_SPARSE])
        row_var = sb("row_var", [P, 8])
        row_std = sb("row_std", [P, 8])
        row_inv = sb("row_inv", [P, 8])
        eye_sb = sb("eye_sb", [P, P])
        ones_sb = sb("ones_sb", [P, P])
        eps_sb = sb("eps_sb", [P, 1])
        mask_sb = sb("mask_sb", [P, CHUNK_TILES, SPAN])
        wsi_sb = sb("wsi_sb", [P, CHUNK_TILES, PROJ])
        ws_mean = sb("ws_mean", [P, 1])
        wsi_mean = sb("wsi_mean", [P, CHUNK_TILES])
        wd_mean = sb("wd_mean", [P, D_CH])
        wl_mean = sb("wl_mean", [P, STEPS])
        wss_h = sb("wss_h", [P, PROJ], f32r)
        wss_l = sb("wss_l", [P, PROJ])
        pat_h = sb("pat_h", [P, CHUNK_TILES, SPAN, PROJ], f32r)
        pat_l = sb("pat_l", [P, CHUNK_TILES, SPAN, PROJ], f32r)
        ws2 = sb("ws2", [P, E_DIM])
        gs_sb = sb("gs_sb", [P, E_DIM])
        bs_sb = sb("bs_sb", [P, E_DIM])
        pick_sb = sb("pick_sb", [P, 2])
        ws_g = sb("ws_g", [P, E_DIM])
        ws_h = sb("ws_h", [P, E_DIM], f32r)
        ws_l = sb("ws_l", [P, E_DIM], f32r)
        ws_b = sb("ws_b", [P, E_DIM], f32r)
        bs_h = sb("bs_h", [P, E_DIM], f32r)
        bs_t = sb("bs_t", [P, E_DIM])
        bs_u = sb("bs_u", [P, E_DIM])
        ws_e = sb("ws_e", [P, P])
        gram = sb("gram", [P, P])
        wd_sb = sb("wd_sb", [P, D_CH, E_DIM])
        dense_mem = sb("dense_mem", [P, 2, D_CH * BODY])
        dense_sb = [dense_mem[:, h].rearrange("p (m n) -> p m n", m=D_CH) for h in range(2)]
        x_dense = dense_mem[:].rearrange("p h w -> p (h w)").rearrange("p (m n) -> p m n", m=D_CH)
        x_sq = prod[:]
        x_t = sb("x_t", [P, BATCH])
        lines = sb("lines", [P, BATCH])
        x_sum = lines[64:65, :]
        y_out = lines[0:1, :]
        gd_sb = sb("gd_sb", [P, 1])
        bd_sb = sb("bd_sb", [P, 1])
        u_h = [sb(f"u_h{h}", [P, UNIT, PROJ], f32r) for h in range(2)]
        u_l = [sb(f"u_l{h}", [P, UNIT, PROJ], f32r) for h in range(2)]
        y_sq = sb("y_sq", [P, UNIT, PROJ])
        y_sum = sb("y_sum", [P, UNIT])
        y_std = sb("y_std", [P, UNIT])
        y_inv = sb("y_inv", [P, UNIT])
        items = [sb(f"items{h}", [P, UNIT, ITEMS]) for h in range(2)]
        pair_words = ITEMS * BODY // 4
        pair_mem = sb("pair_mem", [P, 2 * pair_words])
        pairs = [pair_mem[:, h * pair_words:(h + 1) * pair_words].rearrange("p (q n) -> p q n", q=ITEMS)
                 for h in range(2)]
        pat_words = CHUNK_TILES * SPAN * PROJ
        pat = pair_mem[:, 0:pat_words].rearrange("p (t s q) -> p t s q", t=CHUNK_TILES, s=SPAN)
        ids_f, ids_g = [pair_mem[:, pat_words + h * BLOCKS * TILES:pat_words + (h + 1) * BLOCKS * TILES]
                        for h in range(2)]
        packed = sb("packed", [P, STEPS, BODY])
        packed_h = sb("packed_h", [P, STEPS, BODY], f32r)
        packed_l = sb("packed_l", [P, STEPS, BODY], f32r)
        x_var = sb("x_var", [P, X_CHUNK // P])
        x_std = sb("x_std", [P, X_CHUNK // P])
        x_inv = sb("x_inv", [P, X_CHUNK // P])
        wl_h = sb("wl_h", [P, STEPS, MAXD], f32r)
        wl_l = sb("wl_l", [P, STEPS, MAXD], f32r)
        ga_sb = sb("ga_sb", [P, STEPS])
        gb_sb = sb("gb_sb", [P, STEPS])
        fac = sb("fac", [P, STEPS])
        bc_sb = sb("bc_sb", [P, 1])
        bp_sb = sb("bp_sb", [P, STEPS])
        bq_sb = sb("bq_sb", [P, STEPS])
        sel_mem = sb("sel_mem", [P, 4, STEPS, PROJ])
        selp_sb, selq_sb, sel_a, sel_b = [sel_mem[:, n] for n in range(4)]
        cs_sb = lines
        o_mem = sb("o_mem", [P, 2, BODY])
        o_std, o_inv = o_mem[:, 0], o_mem[:, 1]
        x_rows = o_mem[:].rearrange("p h n -> p (h n)")
        head_mem = sb("head_mem", [P, (O_CH + 2 * Z_CH + 4 + H2_CH) * BODY])
        head_rows = head_mem[:].rearrange("p (c n) -> p c n", n=BODY)
        at = 0
        head_parts = []
        for n in (O_CH, Z_CH, Z_CH, 4, H2_CH):
            head_parts.append(head_rows[:, at:at + n, :])
            at += n
        o_sq, o_sb, z_sb, h1_sb, h2_sb = head_parts
        wl_sb = head_mem[:, 0:STEPS * MAXD].rearrange("p (s o) -> p s o", s=STEPS)
        gl_sb = sb("gl_sb", [P, Z_CH])
        bl_sb = sb("bl_sb", [P, Z_CH])
        w1_sb = sb("w1_sb", [P, Z_CH + D_CH, H1])
        b1_sb = sb("b1_sb", [P, 4])
        b1f = sb("b1f", [P, 4])
        w2_sb = sb("w2_sb", [P, 4, H2])
        b2_sb = sb("b2_sb", [P, H2_CH])
        w3_sb = sb("w3_sb", [P, H2_CH])

        front_ps = ps("front_ps", [P, 512])
        u_ps = ps("u_ps", [P, 2, 512])
        y_ps = ps("y_ps", [P, 2, 512])
        z_ps = ps("z_ps", [P, 512])
        head_ps = ps("head_ps", [P, 4, BODY])

        w_in = [sem(f"w_in{n}") for n in range(6)]
        dense_in = [sem(f"dense_in{c}") for c in range(4)]
        head_in = [sem(f"head_in{h}") for h in range(2)]
        ids_ready = sem("ids_ready")
        idx_copied = sem("idx_copied")
        gathered = [[sem(f"gath{h}{v}") for v in range(4)] for h in range(2)]
        zeroed = sem("zeroed")
        prep = sem("prep")
        prep_pe = sem("prep_pe")
        prep_act = sem("prep_act")
        sums = sem("sums")
        wl_sum = sem("wl_sum")
        wl_centred = sem("wl_centred")
        wl_scaled = sem("wl_scaled")
        wl_prep = sem("wl_prep")
        wl_pe = sem("wl_pe")
        wl_act = sem("wl_act")
        x_pe = sem("x_pe")
        x_sqd = sem("x_sqd")
        x_summed = sem("x_summed")
        x_stdd = sem("x_stdd")
        x_invd = sem("x_invd")
        x_nrm = sem("x_nrm")
        x_turned = sem("x_turned")
        x_done = sem("x_done")
        xs_pe = sem("xs_pe")
        xs_done = sem("xs_done")
        turned = sem("turned")
        turned_sb = sem("turned_sb")
        gram_done = sem("gram_done")
        gram_prod = sem("gram_prod")
        gram_sum = sem("gram_sum")
        row_stdd = sem("row_stdd")
        row_invd = sem("row_invd")
        rows_scaled = sem("rows_scaled")
        rows_high = sem("rows_high")
        rows_low = sem("rows_low")
        u_done = sem("u_done")
        u_high = sem("u_high")
        u_low = sem("u_low")
        y_done = sem("y_done")
        y_squared = sem("y_squared")
        y_summed = sem("y_summed")
        y_stdd = sem("y_stdd")
        y_invd = sem("y_invd")
        x_put = sem("x_put")
        items_done = sem("items_done")
        z_done = sem("z_done")
        pairs_done = sem("pairs_done")
        spilled = sem("spilled")
        repacked = sem("repacked")
        packed_high = sem("packed_high")
        packed_low = sem("packed_low")
        sum_put = sem("sum_put")
        o_done = sem("o_done")
        o_squared = sem("o_squared")
        o_added = sem("o_added")
        ov_done = sem("ov_done")
        o_stdd = sem("o_stdd")
        o_invd = sem("o_invd")
        zn_done = sem("zn_done")
        h1_done = sem("h1_done")
        h1_relu = sem("h1_relu")
        h2_done = sem("h2_done")
        h2_relu = sem("h2_relu")
        yo_done = sem("yo_done")
        yo_copied = sem("yo_copied")
        stored = sem("stored")

        def wait(eng, s, value):
            if not isinstance(value, int) or value > 0:
                eng.wait_ge(s, value)

        block = ctx.enter_context(nc.Block())

        def passes(eng, body):
            body(0, 0)
            body(1, 1)
            with eng.Fori(1, PASSES // 2 - 1) as n:
                body(2 * n, 0)
                body(2 * n + 1, 1)
            body(PASSES - 2, 0)
            body(PASSES - 1, 1)

        def at_end(i):
            return isinstance(i, int) and i == PASSES - 1

        def at_start(i):
            return isinstance(i, int) and i == 0


        x_slots = {0: 1, 3: 2, 8: 3}
        halves = [slice(0, STEPS // 2), slice(STEPS // 2, STEPS)]

        def prepares(i):
            return isinstance(i, int) and i < 2

        def place(c):
            return 2 * (c % 2) + c // 2

        def heads(i):
            return tuple(i - back if not isinstance(i, int) or i >= back else None for back in (1, 2))

        def head_rest(early, late):
            for last, before in ((None, PASSES - 2), (PASSES - 1, None), (None, PASSES - 1)):
                for s in range(SLOTS):
                    early(last, before, (before or 0) % 2, s)
                    late(last, before, (before or 0) % 2, s)

        @block.sync
        def _(sp):
            def load(s, dst, src):
                sp.dma_start(dst, src).then_inc(s, 16)

            load(w_in[0], ids_raw[:], ids)
            load(w_in[0], size_sb[:], size_c)
            load(w_in[0], base_sb[:], base_c)
            load(w_in[1], ws2[:], wst2)
            load(w_in[1], eye_sb[:], eye)
            load(w_in[1], wsi_sb[:], wsi13)
            load(w_in[1], mask_sb[:], mask13)
            load(w_in[2], wd_sb[:], wdt)
            load(dense_in[0], x_dense, dense[:, :, 0:X_CHUNK])
            load(w_in[2], gs_sb[:], gs_b)
            load(w_in[2], bs_sb[:], bs_b)
            load(w_in[2], pick_sb[:], bs_pick)
            load(w_in[2], gd_sb[:], gd_c)
            load(w_in[2], bd_sb[:], bd_c)
            load(w_in[3], wl_sb[:], wl)
            load(w_in[3], ga_sb[:], ga)
            load(w_in[3], gb_sb[:], gb)
            load(w_in[3], bc_sb[:], bsi_c)
            load(w_in[3], bp_sb[:], bsi_p)
            load(w_in[3], bq_sb[:], bsi_q)
            load(w_in[3], selp_sb, sel_p)
            load(w_in[3], selq_sb, sel_q)
            load(w_in[4], w1_sb[:], w1)
            load(w_in[4], gl_sb[:], gl_c)
            load(w_in[4], bl_sb[:], bl_c)
            load(w_in[4], b1_sb[:], b1_c)
            load(w_in[5], w2_sb[:], w2)
            load(w_in[5], b2_sb[:], b2_c)
            load(w_in[5], w3_sb[:], w3)
            for c in range(1, X_CHUNKS):
                sp.wait_ge(x_pe, c)
                load(dense_in[c], x_dense, dense[:, :, c * X_CHUNK:(c + 1) * X_CHUNK])

            def repack(i, par):
                if at_start(i):
                    sp.wait_ge(x_pe, X_CHUNKS)
                sp.wait_ge(pairs_done, 8 * i + 8)
                load(head_in[par], dense_sb[par], dense[:, :, bass.ds(i * BODY, BODY)])
                wait(sp, packed_low, 3 * i)
                for j in range(4):
                    sp.dma_start(spill[par, :, :, 64 * j:64 * j + 64].rearrange("q p n -> p q n"),
                                 pairs[par][32 * j:32 * j + 32]).then_inc(spilled, 16)
                sp.wait_ge(spilled, 64 * i + 64)
                for p0, q0, nq, step0, row0 in STRIPS:
                    sp.dma_start(packed[row0:row0 + PROJ - p0, step0:step0 + nq, :],
                                 spill[par, 1 + q0:1 + q0 + nq, p0:PROJ].rearrange("q p n -> p q n")
                                 ).then_inc(repacked, 16)
                for row0, q in ((0, 0), (PROJ, ITEMS - 1)):
                    sp.dma_start(packed[row0:row0 + PROJ, LAST, :], spill[par, q]).then_inc(repacked, 16)

            sp.wait_ge(zeroed, 8)
            passes(sp, repack)
            sp.wait_ge(yo_copied, PASSES)
            sp.dma_start(out, y_out[:]).then_inc(stored, 16)
            sp.wait_ge(stored, 16)

        @block.gpsimd
        def _(pool):
            def gather(i, h):
                wait(pool, rows_scaled, 8 * i + 4 * h - 4)
                pool.tensor_copy(idx[h][:], idx_all[:, bass.ds((2 * i + h) * TILES, TILES)]).then_inc(idx_copied, 1)
                pool.wait_ge(idx_copied, 2 * i + h + 1)
                pool.nop(nofuse=True)
                for v, (lo, hi) in enumerate(GROUPS):
                    for t in range(lo, hi):
                        pool.indirect_dma_start(
                            rows[h][:, t, :], None, table,
                            bass.IndirectOffsetOnAxis(ap=idx[h][:, t:t + 1], axis=0)).then_inc(gathered[h][v], 16)

            pool.wait_ge(ids_ready, 7)
            gather(0, 0)
            gather(0, 1)
            with pool.Fori(1, PASSES) as i:
                gather(i, 0)
                gather(i, 1)

        @block.tensor
        def _(pe):
            def transposes(q, k_par, v):
                lo, hi = GROUPS[v]
                n = (hi - lo) // 2
                wait(pe, gram_prod, q)
                for m in range(n):
                    src = rows[k_par][:, lo + 2 * m:lo + 2 * m + 2, :].rearrange("p a d -> p (a d)")
                    ins = nc.tensor.transpose(front_ps[:, m * P:(m + 1) * P], src, eye_sb[:])
                ins.then_inc(turned, 1)

            def gram_mm(q, v):
                lo, hi = GROUPS[v]
                pe.wait_ge(turned_sb, q + 1)
                for m in range((hi - lo) // 2):
                    ins = nc.tensor.matmul(front_ps[:, m * P:(m + 1) * P], rows_t[:, m * P:(m + 1) * P], gram[:],
                                           start=True, stop=True)
                ins.then_inc(gram_done, 1)

            def u_mm(u, v):
                pe.wait_ge(rows_low, u + 1)
                wait(pe, u_low, u)
                ch, w = v // 2, v % 2
                for x in range(UNIT // BANK_B):
                    b0 = w * UNIT + x * BANK_B
                    fresh = True
                    for t in range(CHUNK_TILES):
                        lo, hi = max(tile_first(t), b0), min(tile_last(t) + 1, b0 + BANK_B)
                        if lo >= hi:
                            continue
                        both = rows_s[:, ch * CHUNK_TILES + t, :, :].rearrange("p a d -> p (a d)")
                        for part in (pat_h, pat_l):
                            ins = nc.tensor.matmul(
                                u_ps[:, x, (lo - b0) * PROJ:(hi - b0) * PROJ], both,
                                part[:, t, lo - tile_first(t):hi - tile_first(t), :].rearrange("p s q -> p (s q)"),
                                start=fresh, stop=True, skip_group_check=True)
                            fresh = False
                ins.then_inc(u_done, 1)

            def y_mm(u, par):
                pe.wait_ge(u_low, u + 1)
                wait(pe, items_done, u)
                for x in range(UNIT // BANK_B):
                    cut = slice(x * BANK_B, (x + 1) * BANK_B)
                    high = u_h[par][:, cut, :].rearrange("p b q -> p (b q)")
                    low = u_l[par][:, cut, :].rearrange("p b q -> p (b q)")
                    nc.tensor.matmul(y_ps[:, x, :], ws_h[:], high, start=True, stop=False)
                    nc.tensor.matmul(y_ps[:, x, :], ws_l[:], high, start=False, stop=False)
                    ins = nc.tensor.matmul(y_ps[:, x, :], ws_b[:], low, start=False, stop=True)
                ins.then_inc(y_done, 1)

            def z_mm(u, par):
                pe.wait_ge(items_done, u + 1)
                pe.wait_ge(x_put, u + 1)
                wait(pe, pairs_done, u)
                for g in range(GSLOTS):
                    for j in range(4):
                        t = items[par][:, j * GSLOTS + g, :]
                        ins = nc.tensor.matmul(z_ps[32 * j:32 * j + 32, g * ITEMS:(g + 1) * ITEMS],
                                               t[:, 1:1 + PROJ], t, start=True, stop=True)
                ins.then_inc(z_done, 1)

            def o_mm(i, piece):
                if piece == 0:
                    pe.wait_ge(packed_low, 3 * i + 3)
                    wait(pe, yo_copied, i)
                todo = [(c, st) for c in range(O_CH) for st in range(STEPS)]
                size = -(-len(todo) // 5)
                for c, st in todo[piece * size:(piece + 1) * size]:
                    if c >= 2 and st == 0:
                        pe.wait_ge(o_squared, O_CH * i + c - 1)
                    for m, (w, x) in enumerate(((wl_h, packed_h), (wl_l, packed_h), (wl_h, packed_l))):
                        ins = nc.tensor.matmul(head_ps[:, place(c), :], w[:, st, c * P:(c + 1) * P], x[:, st, :],
                                               start=(st == 0 and m == 0), stop=(st == LAST and m == 2))
                    if st == LAST:
                        ins.then_inc(o_done, 1)

            def ov_mm(i):
                pe.wait_ge(o_squared, O_CH * (i + 1))
                pe.wait_ge(o_added, 2 * (i + 1))
                for c in (0, O_CH - 1):
                    ins = nc.tensor.matmul(head_ps[:, place(Z_CH), :], ones_sb[:], o_sq[:, c, :],
                                           start=(c == 0), stop=(c == O_CH - 1))
                ins.then_inc(ov_done, 1)

            def h1_mm(i, par, c, parts):
                if c < 2 and parts[0] == 0:
                    pe.wait_ge(o_stdd, i + 1)
                    pe.wait_ge(head_in[par], (i - par + 2) * 8)
                elif parts[0] == 0:
                    pe.wait_ge(h1_relu, 4 * i + c - 1)
                else:
                    pe.wait_ge(zn_done, i + 1)
                for n in parts:
                    m = (n + Z_CH) % (Z_CH + D_CH)
                    x = z_sb[:, m, :] if m < Z_CH else dense_sb[par][:, m - Z_CH, :]
                    ins = nc.tensor.matmul(head_ps[:, place(c), :], w1_sb[:, m, c * P:(c + 1) * P], x,
                                           start=(n == 0), stop=(n == Z_CH + D_CH - 1))
                if parts[-1] == Z_CH + D_CH - 1:
                    ins.then_inc(h1_done, 1)

            def h2_mm(i, c):
                if c == 0:
                    pe.wait_ge(h1_relu, 4 * (i + 1))
                for m in range(4):
                    ins = nc.tensor.matmul(head_ps[:, place(c), :], w2_sb[:, m, c * P:(c + 1) * P], h1_sb[:, m, :],
                                           start=(m == 0), stop=(m == 3))
                ins.then_inc(h2_done, 1)

            def yo_mm(i):
                pe.wait_ge(h2_relu, i + 1)
                for m in range(H2_CH):
                    ins = nc.tensor.matmul(head_ps[0:1, 2, :], w3_sb[:, m:m + 1], h2_sb[:, m, :],
                                           start=(m == 0), stop=(m == H2_CH - 1))
                ins.then_inc(yo_done, 1)

            x_proj = head_ps[:, 0:2, :].rearrange("p a n -> p (a n)")
            x_back = head_ps[:, 2:4, :].rearrange("p a n -> p (a n)")

            def x_mm(c):
                pe.wait_ge(dense_in[c], 16)
                wait(pe, xs_done, c)
                if c == X_CHUNKS - 1:
                    pe.wait_ge(wl_prep, 6)
                for b in range(X_CHUNK // P):
                    for m in range(D_CH):
                        ins = nc.tensor.matmul(x_proj[:, b * P:(b + 1) * P], x_dense[:, m, b * P:(b + 1) * P],
                                               wd_sb[:, m, :], start=(m == 0), stop=(m == D_CH - 1))
                ins.then_inc(x_pe, 1)

            def x_turn(c):
                pe.wait_ge(x_nrm, c + 1)
                for b in range(X_CHUNK // P):
                    ins = nc.tensor.transpose(x_back[:, b * P:(b + 1) * P], x_rows[:, b * P:(b + 1) * P], eye_sb[:])
                ins.then_inc(x_turned, 1)

            def x_sum_mm(c):
                pe.wait_ge(x_done, c + 1)
                nc.tensor.matmul(x_proj[64:65, :], ones_sb[:, 0:1], x_t[:, c * X_CHUNK:(c + 1) * X_CHUNK],
                                 start=True, stop=True).then_inc(xs_pe, 1)

            def head_early(last, before, par, s):
                if before is not None:
                    if s == 0:
                        h1_mm(before, par, 0, (0, 1))
                    elif s == 1:
                        h1_mm(before, par, 0, (2, 3, 4))
                    elif s == 2:
                        h1_mm(before, par, 2, (0, 1, 2, 3, 4))
                    elif s == 3:
                        h1_mm(before, par, 3, (2, 3, 4))
                    elif s == 4:
                        h2_mm(before, 1)
                if last is not None:
                    if s >= 5:
                        o_mm(last, 2 * (s - 5))

            def head_late(last, before, par, s):
                if before is not None:
                    if s == 0:
                        h1_mm(before, par, 1, (0, 1))
                    elif s == 1:
                        h1_mm(before, par, 1, (2, 3, 4))
                    elif s == 2:
                        h1_mm(before, par, 3, (0, 1))
                    elif s == 3:
                        h2_mm(before, 0)
                    elif s == 4:
                        yo_mm(before)
                if last is not None:
                    if s in (5, 6):
                        o_mm(last, 2 * (s - 5) + 1)
                    elif s == 7:
                        ov_mm(last)

            def prepare_slot(t):
                wide = [head_ps[32:64, 0:2, :], head_ps[64:65, 2:4, :], head_ps[96:97, 0:2, :]]
                coef, x_coef, const = [t.rearrange("p a n -> p (a n)") for t in wide]
                if t in x_slots:
                    x_mm(x_slots[t])
                elif t - 1 in x_slots:
                    x_turn(x_slots[t - 1])
                elif t - 2 in x_slots:
                    x_sum_mm(x_slots[t - 2])
                if t == 6:
                    pe.wait_ge(wl_centred, 2)
                    pe.wait_ge(wl_prep, 3)
                    pe.wait_ge(xs_done, 3)
                    for st in range(STEPS):
                        ins = nc.tensor.matmul(coef, sel_b[:, st, :], wl_sb[:, st, :],
                                               start=(st == 0), stop=(st == LAST))
                    ins.then_inc(wl_pe, 1)
                    nc.tensor.matmul(x_coef, bc_sb[0:32, :], wl_sb[0:32, LAST, :],
                                     start=True, stop=True).then_inc(wl_pe, 1)
                elif t == 7:
                    pe.wait_ge(wl_prep, 4)
                    nc.tensor.matmul(const, bc_sb[32:64, :], cs_sb[32:64, 0:MAXD],
                                     start=True, stop=True).then_inc(wl_pe, 1)
                elif t in (10, 11):
                    if t == 10:
                        pe.wait_ge(w_in[4], 4 * 16)
                        pe.wait_ge(x_done, X_CHUNKS)
                    for c in (0, 1) if t == 10 else (2, 3):
                        for m in range(Z_CH):
                            ins = nc.tensor.matmul(head_ps[:, 2, c:c + 1], w1_sb[:, m, c * P:(c + 1) * P],
                                                   bl_sb[:, m:m + 1], start=(m == 0), stop=(m == Z_CH - 1))
                    ins.then_inc(wl_pe, 1)

            def body(i, par):
                for s in range(SLOTS):
                    u = 8 * i + s
                    ahead = not (at_end(i) and s >= 5)
                    y_mm(u, s % 2)
                    if ahead:
                        v, h = (s + 3) % 4, (s + 3) // 4
                        pe.wait_ge(gathered[h % 2][v], (i + 1 + h // 2) * 16 * (GROUPS[v][1] - GROUPS[v][0]))
                        transposes(u + 3, h % 2, v)
                    if not (at_end(i) and s == SLOTS - 1):
                        u_mm(u + 1, (s + 1) % 4)
                    head_early(*heads(i), par, s)
                    if prepares(i):
                        prepare_slot(u)
                    if ahead:
                        gram_mm(u + 3, v)
                    head_late(*heads(i), par, s)
                    z_mm(u, s % 2)

            pe.wait_ge(w_in[1], 4 * 16)
            pe.wait_ge(zeroed, 8)
            pe.wait_ge(prep, 2)
            nc.tensor.transpose(y_ps[:, 0, 0:P], ws2[:], eye_sb[:]).then_inc(prep_pe, 1)
            pe.wait_ge(prep, 3)
            nc.tensor.matmul(y_ps[:, 1, 0:P], ws_e[:], ws_e[:], start=True, stop=True).then_inc(prep_pe, 1)
            pe.wait_ge(prep, 7)
            nc.tensor.matmul(u_ps[64:128, 0, 0:PROJ], ones_sb[0:N_SPARSE, 0:64],
                             wsi_sb[0:N_SPARSE, 0, :], start=True, stop=True).then_inc(prep_pe, 1)

            pe.wait_ge(prep, 8)
            def first_group(v):
                pe.wait_ge(gathered[0][v], 16 * (GROUPS[v][1] - GROUPS[v][0]))
                transposes(v, 0, v)
                gram_mm(v, v)

            x_mm(0)
            first_group(0)
            x_turn(0)
            first_group(1)
            pe.wait_ge(prep_act, 4)
            pe.wait_ge(prep, 19)
            u_mm(0, 0)
            x_sum_mm(0)
            first_group(2)

            passes(pe, body)
            head_rest(head_early, head_late)

        @block.scalar
        def _(act):
            def turn_copy(q, v):
                n = (GROUPS[v][1] - GROUPS[v][0]) // 2 * P
                act.wait_ge(turned, q + 1)
                wait(act, gram_done, q)
                nc.scalar.activation(rows_t[:, 0:n], front_ps[:, 0:n], ACT.Copy).then_inc(turned_sb, 1)

            def row_std_f(q, v):
                n = GROUPS[v][1] - GROUPS[v][0]
                act.wait_ge(gram_sum, q + 1)
                wait(act, row_invd, q)
                nc.scalar.activation(row_std[:, 0:n], row_var[:, 0:n], ACT.Sqrt, bias=eps_sb[:],
                                     scale=1.0 / E_DIM).then_inc(row_stdd, 1)

            def rows_high_f(q, v):
                lo, hi = GROUPS[v]
                act.wait_ge(rows_scaled, q + 1)
                wait(act, u_done, q - (2 if v < 3 else 3))
                nc.scalar.activation(rows_s[:, lo:hi, 0, :], rows_f[:, 0:hi - lo, :],
                                     ACT.Copy).then_inc(rows_high, 1)

            def u_high_f(u, par):
                act.wait_ge(u_done, u + 1)
                wait(act, y_done, u - 1)
                nc.scalar.activation(u_h[par][:].rearrange("p b q -> p (b q)"),
                                     u_ps[:].rearrange("p a n -> p (a n)"), ACT.Copy).then_inc(u_high, 1)

            def put_x(u, par, i, h, v):
                wait(act, z_done, u - 1)
                src = x_t[:, bass.ds(i * BODY, BODY)].rearrange("p (j h v g) -> p h v j g", j=4, h=2, v=4)[:, h, v]
                nc.scalar.activation(items[par][:, :, 0].rearrange("p (j g) -> p j g", j=4), src,
                                     ACT.Copy).then_inc(x_put, 1)

            def y_square(u):
                act.wait_ge(y_done, u + 1)
                wait(act, y_summed, u)
                nc.scalar.activation(y_sq[:].rearrange("p b q -> p (b q)"),
                                     y_ps[:].rearrange("p a n -> p (a n)"), ACT.Square).then_inc(y_squared, 1)

            def y_std_f(u):
                act.wait_ge(y_summed, u + 1)
                wait(act, y_invd, u)
                nc.scalar.activation(y_std[:], y_sum[:], ACT.Sqrt, bias=eps_sb[:],
                                     scale=1.0 / PROJ).then_inc(y_stdd, 1)

            def z_copy(u, par, s):
                act.wait_ge(z_done, u + 1)
                nc.scalar.activation(
                    pairs[par][:, :, s * GSLOTS:(s + 1) * GSLOTS].rearrange("p q g -> p g q"),
                    z_ps[:, 0:GSLOTS * ITEMS].rearrange("p (g q) -> p g q", q=ITEMS),
                    ACT.Copy).then_inc(pairs_done, 1)

            def sum_put_f(i):
                nc.scalar.activation(packed[ROW_SUM:ROW_SUM + 1, LAST, :],
                                     x_sum[:, bass.ds(i * BODY, BODY)], ACT.Copy).then_inc(sum_put, 1)

            def packed_high_f(i, part):
                if part == 0:
                    act.wait_ge(repacked, (i + 1) * PACK_DMAS * 16)
                    act.wait_ge(sum_put, i + 1)
                steps = slice(STEPS * part // 3, STEPS * (part + 1) // 3)
                nc.scalar.activation(packed_h[:, steps, :], packed[:, steps, :], ACT.Copy).then_inc(packed_high, 1)

            def o_square(i, c):
                act.wait_ge(o_done, O_CH * i + c + 1)
                ins = nc.scalar.activation(o_sq[:, c, :], head_ps[:, place(c), :], ACT.Square)
                if c < Z_CH:
                    ins = nc.scalar.activation(o_sb[:, c, :], head_ps[:, place(c), :], ACT.Copy)
                ins.then_inc(o_squared, 1)

            def o_std_f(i):
                act.wait_ge(ov_done, i + 1)
                nc.scalar.activation(o_std, head_ps[:, place(Z_CH), :], ACT.Sqrt, bias=eps_sb[:],
                                     scale=1.0 / MAXD).then_inc(o_stdd, 1)

            def h1_act(i, c):
                act.wait_ge(h1_done, 4 * i + c + 1)
                nc.scalar.activation(h1_sb[:, c, :], head_ps[:, place(c), :], ACT.Relu, bias=b1f[:, c:c + 1]).then_inc(h1_relu, 1)

            def h2_act(i):
                act.wait_ge(h2_done, H2_CH * (i + 1))
                for c in range(H2_CH):
                    ins = nc.scalar.activation(h2_sb[:, c, :], head_ps[:, place(c), :], ACT.Relu, bias=b2_sb[:, c:c + 1])
                ins.then_inc(h2_relu, 1)

            def yo_copy(i):
                act.wait_ge(yo_done, i + 1)
                nc.scalar.activation(y_out[:, bass.ds(i * BODY, BODY)], head_ps[0:1, 2, :],
                                     ACT.Copy).then_inc(yo_copied, 1)

            def head_early(last, before, par, s):
                if before is not None:
                    if s == 0:
                        o_std_f(before)
                    elif s == 2:
                        h1_act(before, 1)
                    elif s == 5:
                        yo_copy(before)
                if last is not None:
                    if s == 0:
                        sum_put_f(last)
                    elif s == 3:
                        packed_high_f(last, 0)
                    elif s == 4:
                        packed_high_f(last, 2)
                    elif s == 6:
                        o_square(last, 0)
                    elif s == 7:
                        o_square(last, 2)

            def head_late(last, before, par, s):
                if before is not None:
                    if s == 1:
                        h1_act(before, 0)
                    elif s == 2:
                        h1_act(before, 2)
                    elif s == 3:
                        h1_act(before, 3)
                    elif s == 4:
                        h2_act(before)
                if last is not None:
                    if s == 3:
                        packed_high_f(last, 1)
                    elif s == 6:
                        o_square(last, 1)
                    elif s == 7:
                        o_square(last, 3)

            def prepare_slot(t):
                if t in x_slots:
                    x_square(x_slots[t])
                elif t - 1 in x_slots:
                    x_copy(x_slots[t - 1])
                elif t - 2 in x_slots:
                    x_sum_copy(x_slots[t - 2])
                if t in (2, 3):
                    act.wait_ge(wl_sum, 4)
                    for st in range(STEPS)[halves[t - 2]]:
                        ins = nc.scalar.activation(wl_sb[:, st, :], wl_sb[:, st, :], ACT.Identity,
                                                   bias=wl_mean[:, st:st + 1])
                    ins.then_inc(wl_centred, 1)
                elif t == 6:
                    act.wait_ge(wl_pe, 2)
                    for st in range(STEPS):
                        ins = nc.scalar.activation(wl_sb[:, st, :], wl_sb[:, st, :], ACT.Copy,
                                                   scale=fac[:, st:st + 1])
                    ins.then_inc(wl_scaled, 1)
                elif t in (8, 9):
                    act.wait_ge(wl_prep, 6)
                    nc.scalar.activation(wl_h[:, halves[t - 8], :], wl_sb[:, halves[t - 8], :],
                                         ACT.Copy).then_inc(wl_act, 1)

            def body(i, par):
                for s in range(SLOTS):
                    u = 8 * i + s
                    split = not (at_end(i) and s >= 6)
                    head_early(*heads(i), par, s)
                    if prepares(i) and u - 1 in x_slots:
                        x_std_f(x_slots[u - 1])
                    if not (at_start(i) and s == 0):
                        z_copy(u - 1, par if s else 1 - par, (s - 1) % 8)
                    put_x(u, s % 2, i, s // 4, s % 4)
                    if split:
                        row_std_f(u + 2, (s + 2) % 4)
                    y_square(u)
                    if not (at_end(i) and s >= 5):
                        turn_copy(u + 3, (s + 3) % 4)
                    if split:
                        rows_high_f(u + 2, (s + 2) % 4)
                    if not (at_end(i) and s == SLOTS - 1):
                        u_high_f(u + 1, 1 - s % 2)
                    y_std_f(u)
                    head_late(*heads(i), par, s)
                    if prepares(i):
                        prepare_slot(u)

            x_proj = head_ps[:, 0:2, :].rearrange("p a n -> p (a n)")
            x_back = head_ps[:, 2:4, :].rearrange("p a n -> p (a n)")

            def x_square(c):
                act.wait_ge(x_pe, c + 1)
                wait(act, x_summed, c)
                nc.scalar.activation(x_sq, x_proj, ACT.Square).then_inc(x_sqd, 1)

            def x_std_f(c):
                act.wait_ge(x_summed, c + 1)
                wait(act, x_invd, c)
                nc.scalar.activation(x_std[:], x_var[:], ACT.Sqrt, bias=eps_sb[:],
                                     scale=1.0 / E_DIM).then_inc(x_stdd, 1)

            def x_copy(c):
                act.wait_ge(x_turned, c + 1)
                nc.scalar.activation(x_t[:, c * X_CHUNK:(c + 1) * X_CHUNK], x_back, ACT.Identity, bias=bd_sb[:],
                                     scale=gd_sb[:]).then_inc(x_done, 1)

            def x_sum_copy(c):
                act.wait_ge(xs_pe, c + 1)
                nc.scalar.activation(x_sum[:, c * X_CHUNK:(c + 1) * X_CHUNK], x_proj[64:65, :],
                                     ACT.Copy).then_inc(xs_done, 1)

            act.wait_ge(zeroed, 8)
            act.wait_ge(w_in[2], 6 * 16)
            nc.scalar.activation(bs_h[:], bs_sb[:], ACT.Copy).then_inc(prep_act, 1)
            act.wait_ge(prep, 6)
            nc.scalar.activation(ws_h[:], ws_g[:], ACT.Copy).then_inc(prep_act, 1)
            act.wait_ge(prep_pe, 3)
            nc.scalar.activation(wss_h[64:128, :], u_ps[64:128, 0, 0:PROJ], ACT.Copy).then_inc(prep_act, 1)
            act.wait_ge(prep, 9)
            nc.scalar.activation(pat_h[:], pat[:], ACT.Copy).then_inc(prep_act, 1)
            x_square(0)
            x_std_f(0)
            turn_copy(0, 0)
            row_std_f(0, 0)
            x_copy(0)
            turn_copy(1, 1)
            rows_high_f(0, 0)
            row_std_f(1, 1)
            rows_high_f(1, 1)
            u_high_f(0, 0)
            x_sum_copy(0)
            turn_copy(2, 2)
            act.wait_ge(w_in[5], 3 * 16)
            passes(act, body)
            z_copy(UNITS * BLOCKS - 1, 1, 7)
            head_rest(head_early, head_late)

        @block.vector
        def _(dve):
            V = nc.vector

            def gram_reduce(q, k_par, v):
                lo, hi = GROUPS[v]
                n = hi - lo
                pr = prod[:, 0:n * D_SPARSE].rearrange("p (t d) -> p t d", d=D_SPARSE)
                dve.wait_ge(gram_done, q + 1)
                V.tensor_tensor(pr, front_ps[:, 0:n * D_SPARSE].rearrange("p (t d) -> p t d", d=D_SPARSE),
                                rows[k_par][:, lo:hi, :], ALU.mult).then_inc(gram_prod, 1)
                dve.wait_ge(gram_prod, q + 1)
                V.tensor_reduce(out=row_var[:, 0:n], in_=pr, axis=AX, op=ALU.add).then_inc(gram_sum, 1)

            def scale_rows(q, k_par, v):
                lo, hi = GROUPS[v]
                n = hi - lo
                dve.wait_ge(row_stdd, q + 1)
                V.reciprocal(row_inv[:, 0:n], row_std[:, 0:n]).then_inc(row_invd, 1)
                dve.wait_ge(row_invd, q + 1)
                wait(dve, rows_low, q)
                V.tensor_tensor(rows_f[:, 0:n, :], rows[k_par][:, lo:hi, :],
                                row_inv[:, 0:n].unsqueeze(2).to_broadcast([P, n, D_SPARSE]),
                                ALU.mult).then_inc(rows_scaled, 1)

            def rows_low_f(q, v):
                lo, hi = GROUPS[v]
                dve.wait_ge(rows_high, q + 1)
                V.tensor_tensor(rows_s[:, lo:hi, 1, :], rows_f[:, 0:hi - lo, :],
                                rows_s[:, lo:hi, 0, :].bitcast(fp32), ALU.subtract).then_inc(rows_low, 1)

            def u_low_f(u, par):
                dve.wait_ge(u_high, u + 1)
                wait(dve, y_done, u - 1)
                V.tensor_tensor(u_l[par][0:64].rearrange("p b q -> p (b q)"),
                                u_ps[0:64].rearrange("p a n -> p (a n)"),
                                u_h[par][0:64].rearrange("p b q -> p (b q)").bitcast(fp32),
                                ALU.subtract).then_inc(u_low, 1)

            def y_reduce(u):
                dve.wait_ge(y_squared, u + 1)
                wait(dve, y_stdd, u)
                V.tensor_reduce(out=y_sum[:], in_=y_sq[:], axis=AX, op=ALU.add).then_inc(y_summed, 1)

            def normalise(u, par):
                dve.wait_ge(y_stdd, u + 1)
                V.reciprocal(y_inv[:], y_std[:]).then_inc(y_invd, 1)
                dve.wait_ge(y_invd, u + 1)
                wait(dve, z_done, u - 1)
                V.tensor_tensor(items[par][:, :, 1:1 + PROJ], y_ps[:].rearrange("p a (b q) -> p (a b) q", q=PROJ),
                                y_inv[:].unsqueeze(2).to_broadcast([P, UNIT, PROJ]), ALU.mult).then_inc(items_done, 1)

            def packed_low_f(i, part):
                dve.wait_ge(packed_high, 3 * i + part + 1)
                steps = slice(STEPS * part // 3, STEPS * (part + 1) // 3)
                V.tensor_tensor(packed_l[:, steps, :], packed[:, steps, :], packed_h[:, steps, :].bitcast(fp32),
                                ALU.subtract).then_inc(packed_low, 1)

            def o_add(i):
                dve.wait_ge(o_squared, O_CH * i + 3)
                V.tensor_tensor(o_sq[:, 0, :], o_sq[:, 0, :], o_sq[:, 1, :], ALU.add).then_inc(o_added, 1)
                dve.wait_ge(o_added, 2 * i + 1)
                V.tensor_tensor(o_sq[:, 0, :], o_sq[:, 0, :], o_sq[:, 2, :], ALU.add).then_inc(o_added, 1)

            def o_inv_f(i, half):
                dve.wait_ge(o_stdd, i + 1)
                cut = slice(half * BODY // 2, (half + 1) * BODY // 2)
                V.reciprocal(o_inv[:, cut], o_std[:, cut]).then_inc(o_invd, 1)

            def z_norm(i):
                dve.wait_ge(o_invd, 2 * (i + 1))
                V.tensor_tensor(z_sb[:], o_sb[:], o_inv.unsqueeze(1).to_broadcast([P, Z_CH, BODY]),
                                ALU.mult).then_inc(zn_done, 1)

            x_proj = head_ps[:, 0:2, :].rearrange("p a n -> p (a n)")

            def x_reduce(c):
                dve.wait_ge(x_sqd, c + 1)
                wait(dve, x_stdd, c)
                V.tensor_reduce(out=x_var[:], in_=x_sq.rearrange("p (b e) -> p b e", e=E_DIM), axis=AX,
                                op=ALU.add).then_inc(x_summed, 1)
                dve.wait_ge(x_summed, c + 1)

            def x_norm(c):
                dve.wait_ge(x_stdd, c + 1)
                V.reciprocal(x_inv[:], x_std[:]).then_inc(x_invd, 1)
                dve.wait_ge(x_invd, c + 1)
                wait(dve, x_turned, c)
                V.tensor_tensor(x_rows.rearrange("p (b e) -> p b e", e=E_DIM),
                                x_proj.rearrange("p (b e) -> p b e", e=E_DIM),
                                x_inv[:].unsqueeze(2).to_broadcast([P, X_CHUNK // P, E_DIM]),
                                ALU.mult).then_inc(x_nrm, 1)

            def head_early(last, before, par, s):
                if before is not None:
                    if s == 0:
                        o_inv_f(before, 0)
                    elif s == 1:
                        z_norm(before)
                if last is not None:
                    if s == 4:
                        packed_low_f(last, 1)
                    elif s == 7:
                        o_add(last)

            def head_late(last, before, par, s):
                if before is not None:
                    if s == 0:
                        o_inv_f(before, 1)
                if last is not None:
                    if s == 3:
                        packed_low_f(last, 0)
                    elif s == 4:
                        packed_low_f(last, 2)

            def prepare_slot(t):
                wide = [head_ps[32:64, 0:2, :], head_ps[64:65, 2:4, :], head_ps[96:97, 0:2, :]]
                coef, x_coef, const = [t.rearrange("p a n -> p (a n)") for t in wide]
                if t in x_slots:
                    x_reduce(x_slots[t])
                if t in (0, 1):
                    dve.wait_ge(w_in[3], 8 * 16)
                    V.tensor_reduce(out=wl_mean[:, halves[t]], in_=wl_sb[:, halves[t], :], axis=AX,
                                    op=ALU.add).then_inc(wl_sum, 1)
                    if t == 1:
                        dve.wait_ge(wl_sum, 2)
                        V.tensor_scalar(wl_mean[:], wl_mean[:], -1.0 / MAXD, None, ALU.mult).then_inc(wl_sum, 1)
                        V.tensor_tensor(fac[:], ga_sb[:], gb_sb[:], ALU.mult).then_inc(wl_sum, 1)
                elif t == 4:
                    sel = [P, STEPS, PROJ]
                    V.tensor_tensor(sel_a, selp_sb, bq_sb[:].unsqueeze(2).to_broadcast(sel),
                                    ALU.mult).then_inc(wl_prep, 1)
                    V.tensor_tensor(sel_b, selq_sb, bp_sb[:].unsqueeze(2).to_broadcast(sel),
                                    ALU.mult).then_inc(wl_prep, 1)
                    dve.wait_ge(wl_prep, 2)
                    V.tensor_tensor(sel_b, sel_b, sel_a, ALU.add).then_inc(wl_prep, 1)
                elif t == 6:
                    dve.wait_ge(wl_pe, 2)
                    V.tensor_copy(cs_sb[32:64, 0:MAXD], coef).then_inc(wl_prep, 1)
                if t == 7:
                    dve.wait_ge(wl_pe, 3)
                    dve.wait_ge(wl_scaled, 1)
                    V.tensor_scalar(wl_sb[32:64, LAST, :], cs_sb[32:64, 0:MAXD], ga_sb[32:64, LAST:STEPS], None, ALU.mult)
                    V.tensor_copy(wl_sb[ROW_SUM:ROW_SUM + 1, LAST, :], x_coef).then_inc(wl_prep, 1)
                    V.tensor_scalar(wl_sb[ROW_ONE:ROW_ONE + 1, LAST, :], const, float(E_DIM) / 2.0, None,
                                    ALU.mult).then_inc(wl_prep, 1)
                elif t in (9, 10):
                    half = halves[t - 9]
                    dve.wait_ge(wl_act, t - 8)
                    V.tensor_tensor(wl_l[:, half, :], wl_sb[:, half, :], wl_h[:, half, :].bitcast(fp32),
                                    ALU.subtract).then_inc(wl_prep, 1)
                elif t == 11:
                    dve.wait_ge(wl_pe, 5)
                    V.tensor_tensor(b1f[:], head_ps[:, 2, 0:4], b1_sb[:], ALU.add).then_inc(wl_prep, 1)
                elif t == 12:
                    V.tensor_tensor(w1_sb[:, 0:Z_CH, :], w1_sb[:, 0:Z_CH, :],
                                    gl_sb[:].unsqueeze(2).to_broadcast([P, Z_CH, H1]), ALU.mult).then_inc(wl_prep, 1)

            def body(i, par):
                for s in range(SLOTS):
                    u = 8 * i + s
                    split = not (at_end(i) and s >= 6)
                    h, v = (s + 2) // 4 % 2, (s + 2) % 4
                    if split:
                        gram_reduce(u + 2, h, v)
                        scale_rows(u + 2, h, v)
                    head_early(*heads(i), par, s)
                    if prepares(i) and u - 1 in x_slots:
                        x_norm(x_slots[u - 1])
                    y_reduce(u)
                    if split:
                        rows_low_f(u + 2, v)
                    normalise(u, s % 2)
                    if not (at_end(i) and s == SLOTS - 1):
                        u_low_f(u + 1, 1 - s % 2)
                    head_late(*heads(i), par, s)
                    if prepares(i):
                        prepare_slot(u)

            V.memset(eps_sb[:], EPS).then_inc(zeroed, 1)
            V.memset(ones_sb[:], 1.0).then_inc(zeroed, 1)
            V.memset(gram[:], 0.0).then_inc(zeroed, 1)
            V.memset(packed[64:128, LAST, :], 0.0).then_inc(zeroed, 1)
            V.memset(packed[96:128, 0:LAST, :], 0.0).then_inc(zeroed, 1)
            V.memset(items[0][:, :, ITEMS - 1], 1.0).then_inc(zeroed, 1)
            V.memset(items[1][:, :, ITEMS - 1], 1.0).then_inc(zeroed, 1)
            dve.wait_ge(zeroed, 7)
            V.memset(packed[ROW_ONE:ROW_ONE + 1, LAST, :], 1.0).then_inc(zeroed, 1)

            dve.wait_ge(w_in[0], 3 * 16)
            three = [P, BLOCKS * 2, CHUNK_TILES]

            def by_tile(t):
                return t.rearrange("p (c t) -> p c t", t=CHUNK_TILES)

            def const(t):
                return t[:].unsqueeze(1).to_broadcast(three)

            V.tensor_scalar(last_sb[:], size_sb[:], -1.0, None, ALU.add).then_inc(ids_ready, 1)
            V.tensor_scalar(ids_f[:], ids_raw[:], 0.0, None, ALU.is_lt).then_inc(ids_ready, 1)
            dve.wait_ge(ids_ready, 2)
            V.tensor_tensor(by_tile(ids_g), by_tile(ids_f), const(size_sb), ALU.mult).then_inc(ids_ready, 1)
            dve.wait_ge(ids_ready, 3)
            V.tensor_tensor(ids_f[:], ids_raw[:], ids_g[:], ALU.add).then_inc(ids_ready, 1)
            dve.wait_ge(ids_ready, 4)
            V.tensor_scalar(ids_g[:], ids_f[:], 0.0, None, ALU.max).then_inc(ids_ready, 1)
            dve.wait_ge(ids_ready, 5)
            V.tensor_tensor(by_tile(ids_f), by_tile(ids_g), const(last_sb), ALU.min).then_inc(ids_ready, 1)
            dve.wait_ge(ids_ready, 6)
            V.tensor_tensor(by_tile(idx_all[:]), by_tile(ids_f), const(base_sb), ALU.add).then_inc(ids_ready, 1)

            dve.wait_ge(w_in[1], 4 * 16)
            V.tensor_reduce(out=ws_mean[:], in_=ws2[:], axis=AX, op=ALU.add).then_inc(sums, 1)
            dve.wait_ge(sums, 1)
            V.tensor_scalar(ws_mean[:], ws_mean[:], 1.0 / E_DIM, None, ALU.mult).then_inc(prep, 1)
            dve.wait_ge(prep, 1)
            V.tensor_scalar(ws2[:], ws2[:], ws_mean[:], None, ALU.subtract).then_inc(prep, 1)
            dve.wait_ge(prep_pe, 1)
            V.tensor_copy(ws_e[:], y_ps[:, 0, 0:P]).then_inc(prep, 1)
            V.tensor_reduce(out=wsi_mean[:], in_=wsi_sb[:], axis=AX, op=ALU.add).then_inc(sums, 1)
            dve.wait_ge(prep_pe, 2)
            V.tensor_copy(gram[0:64, 0:64], y_ps[0:64, 1, 0:64]).then_inc(prep, 1)
            V.tensor_copy(gram[64:128, 64:128], y_ps[64:128, 1, 64:128]).then_inc(prep, 1)
            dve.wait_ge(w_in[2], 6 * 16)
            V.tensor_tensor(ws_g[:], ws2[:], gs_sb[:], ALU.mult).then_inc(prep, 1)

            dve.wait_ge(sums, 2)
            V.tensor_scalar(wsi_mean[:], wsi_mean[:], 1.0 / PROJ, None, ALU.mult).then_inc(sums, 1)
            V.tensor_reduce(out=wd_mean[:], in_=wd_sb[:], axis=AX, op=ALU.add).then_inc(sums, 1)
            dve.wait_ge(sums, 4)
            V.tensor_tensor(wsi_sb[:], wsi_sb[:], wsi_mean[:].unsqueeze(2).to_broadcast(
                [P, CHUNK_TILES, PROJ]), ALU.subtract).then_inc(prep, 1)
            V.tensor_scalar(wd_mean[:], wd_mean[:], 1.0 / E_DIM, None, ALU.mult).then_inc(sums, 1)
            dve.wait_ge(sums, 5)
            V.tensor_tensor(wd_sb[:], wd_sb[:], wd_mean[:].unsqueeze(2).to_broadcast([P, D_CH, E_DIM]),
                            ALU.subtract).then_inc(prep, 1)
            dve.wait_ge(prep, 7)
            four = [P, CHUNK_TILES, SPAN, PROJ]
            V.tensor_tensor(pat[:], wsi_sb[:].unsqueeze(2).to_broadcast(four),
                            mask_sb[:].unsqueeze(3).to_broadcast(four), ALU.mult).then_inc(prep, 1)

            dve.wait_ge(prep_act, 3)
            for h in range(2):
                V.tensor_copy(u_l[h][64:96], wss_h[64:96, :].bitcast(fp32).unsqueeze(1).to_broadcast(
                    [32, UNIT, PROJ])).then_inc(prep, 1)
            V.tensor_tensor(wss_l[64:128, :], u_ps[64:128, 0, 0:PROJ], wss_h[64:128, :].bitcast(fp32),
                            ALU.subtract).then_inc(prep, 1)
            dve.wait_ge(prep, 12)
            for h in range(2):
                V.tensor_copy(u_l[h][96:128], wss_l[96:128, :].unsqueeze(1).to_broadcast(
                    [32, UNIT, PROJ])).then_inc(prep, 1)
            V.tensor_tensor(ws_l[:], ws_g[:], ws_h[:].bitcast(fp32), ALU.subtract).then_inc(prep, 1)
            V.tensor_copy(ws_b[0:64, :], ws_h[0:64, :].bitcast(fp32)).then_inc(prep, 1)
            V.tensor_tensor(bs_t[:], bs_sb[:], bs_h[:].bitcast(fp32), ALU.subtract).then_inc(sums, 1)
            V.tensor_scalar(bs_u[:], bs_h[:].bitcast(fp32), pick_sb[:, 0:1], None, ALU.mult).then_inc(sums, 1)
            dve.wait_ge(sums, 7)
            V.tensor_scalar(bs_t[:], bs_t[:], pick_sb[:, 1:2], None, ALU.mult).then_inc(prep, 1)
            dve.wait_ge(prep, 17)
            V.tensor_tensor(ws_b[64:128, :], bs_t[64:128, :], bs_u[64:128, :], ALU.add).then_inc(prep, 1)
            x_reduce(0)
            dve.wait_ge(prep_act, 4)
            V.tensor_tensor(pat_l[:], pat[:], pat_h[:].bitcast(fp32), ALU.subtract).then_inc(prep, 1)
            x_norm(0)

            gram_reduce(0, 0, 0)
            scale_rows(0, 0, 0)
            rows_low_f(0, 0)
            gram_reduce(1, 0, 1)
            scale_rows(1, 0, 1)
            rows_low_f(1, 1)
            u_low_f(0, 0)

            passes(dve, body)
            head_rest(head_early, head_late)




def kernel(**inputs):
    import numpy as np
    import concourse.bacc as bacc
    from concourse import mybir as _mybir
    from concourse.bass_utils import run_bass_kernel_spmd as run

    a = {k: np.asarray(v) for k, v in inputs.items()}
    f32 = np.float32
    tile_rows = np.arange(CHUNK * N_SPARSE).reshape(CHUNK_TILES, P).T
    of_table, of_sample = tile_rows % N_SPARSE, tile_rows // N_SPARSE
    sizes = np.array([a[f"tbl_{n}"].shape[0] for n in range(N_SPARSE)])
    firsts = np.concatenate([[0], np.cumsum(sizes)[:-1]])
    first_of = np.array([tile_first(t) for t in range(CHUNK_TILES)])
    mask = (of_sample - first_of)[:, :, None] == np.arange(SPAN)[None, None, :]

    part = np.arange(P)
    p_of = np.zeros((P, STEPS), int)
    q_of = np.zeros((P, STEPS), int)
    valid = np.zeros((P, STEPS), bool)
    for p0, q0, nq, step0, row0 in STRIPS:
        n = PROJ - p0
        p_of[row0:row0 + n, step0:step0 + nq] = p0 + np.arange(n)[:, None]
        q_of[row0:row0 + n, step0:step0 + nq] = q0 + np.arange(nq)[None, :]
        valid[row0:row0 + n, step0:step0 + nq] = True
    valid &= p_of > q_of
    wl_t = a["L0_rec_Wl"].T
    wl = np.zeros((P, STEPS, MAXD), f32)
    wl[valid] = wl_t[((p_of + 1) * p_of // 2 + q_of + 1)[valid]]
    one = np.arange(PROJ)
    wl[0:PROJ, LAST, :] = wl_t[(one + 1) * one // 2]
    gsi, bsi = a["L0_rec_gsi"], a["L0_rec_bsi"]
    ga = gsi[p_of]
    gb = gsi[q_of]
    ga[0:2 * PROJ, LAST] = gsi[part[0:2 * PROJ] % PROJ]
    gb[0:2 * PROJ, LAST] = 1.0
    place = valid[:, :, None]
    bs_pick = np.zeros((P, 2), f32)
    bs_pick[64, 0] = bs_pick[96, 0] = bs_pick[65, 1] = 1.0
    dense_t = a["r_dense_t"].T.reshape(D_CH, P, PASSES, 2, UNITS, 4, GSLOTS).transpose(1, 0, 2, 5, 3, 4, 6)
    w1 = a["W_top1"].reshape(6, P, H1).transpose(1, 0, 2)[:, [0, 1, 2, 4, 5]]

    given = {
        "table": np.concatenate([a[f"tbl_{n}"] for n in range(N_SPARSE)], axis=0),
        "ids": a["ids"].reshape(BLOCKS * TILES, P).T,
        "dense": dense_t.reshape(P, D_CH, BATCH),
        "size_c": sizes[of_table].astype(f32),
        "base_c": firsts[of_table].astype(f32),
        "eye": np.eye(P, dtype=f32),
        "mask13": mask.astype(f32),
        "sel_p": ((p_of[:, :, None] == one) & place).astype(f32),
        "sel_q": ((q_of[:, :, None] == one) & place).astype(f32),
        "wst2": np.concatenate([a["L0_rec_Ws"].T] * 2, axis=0),
        "gs_b": np.broadcast_to(a["L0_rec_gs"], (P, E_DIM)),
        "bs_b": np.broadcast_to(a["L0_rec_bs"], (P, E_DIM)),
        "bs_pick": bs_pick,
        "wdt": a["L0_rec_Wd"].T.reshape(D_CH, P, E_DIM).transpose(1, 0, 2),
        "gd_c": a["L0_rec_gd"].reshape(P, 1),
        "bd_c": a["L0_rec_bd"].reshape(P, 1),
        "wsi13": a["L0_rec_Wsi"].T[of_table],
        "wl": wl, "ga": ga, "gb": gb,
        "bsi_c": bsi[part % PROJ].reshape(P, 1),
        "bsi_p": bsi[p_of],
        "bsi_q": bsi[q_of],
        "gl_c": a["L0_rec_gl"][0:DIMS_IN_USE].reshape(Z_CH, P).T,
        "bl_c": a["L0_rec_bl"][0:DIMS_IN_USE].reshape(Z_CH, P).T,
        "w1": w1,
        "b1_c": a["b_top1"].reshape(4, P).T,
        "w2": a["W_top2"].reshape(4, P, H2).transpose(1, 0, 2),
        "b2_c": a["b_top2"].reshape(H2_CH, P).T,
        "w3": a["W_top3"].reshape(H2_CH, P).T,
    }
    nc = bacc.Bacc("TRN2", target_bir_lowering=False, num_devices=1)
    arrays, args = {}, {}
    for name, v in given.items():
        v = np.ascontiguousarray(v)
        arrays[f"in_{name}"] = v
        args[name] = nc.dram_tensor(f"in_{name}", v.shape, _mybir.dt.from_np(v.dtype), kind="ExternalInput").ap()
    out = nc.dram_tensor("out_y", (1, BATCH), _mybir.dt.float32, kind="ExternalOutput").ap()
    spill = nc.dram_tensor("spill", (2, ITEMS, PROJ, BODY), _mybir.dt.float32, kind="Internal").ap()
    build_program(nc, spill=spill, out=out, **args)
    r = run(nc, [arrays], core_ids=[0])
    y = r.results[0]["out_y"].reshape(PASSES, 4, 2, UNITS, GSLOTS).transpose(0, 2, 3, 1, 4)
    return y.reshape(BATCH, 1)
```
